# Optimizing a Trainium2 kernel written in Bass

```python
import numpy as np
import jax
import jax.numpy as jnp

def _softmax(x, axis=-1):
    return jax.nn.softmax(x, axis=axis)

def _gelu(x):
    return jax.nn.gelu(x, approximate=True)

def _silu(x):
    return jax.nn.silu(x)

def _sigmoid(x):
    return jax.nn.sigmoid(x)

def _layernorm(x, axis=-1, eps=1e-05):
    m = jnp.mean(x, axis=axis, keepdims=True)
    v = jnp.var(x, axis=axis, keepdims=True)
    return (x - m) / jnp.sqrt(v + eps)

def _scatter_add(tgt, idx, src, axis=0):
    return tgt.at[idx].add(src)

def _segment_sum(src, seg, n):
    return jax.ops.segment_sum(src, seg, n)
kernel_name = 'mk_vit_tower_d1_tok_img768_r4_0978e2'

def setup_inputs(seed: int=0):
    np.random.seed(seed)
    _w = jnp.asarray

    def _rec_inputs():
        import jax
        import jax.numpy as jnp
        _rk = jax.random.key(seed)
        x = -0.000356955 + 1 * jax.random.normal(jax.random.fold_in(_rk, 1), (64, 3, 224, 224), jnp.float32)
        return x
    x = _rec_inputs()

    def _L0_tok_setup():
        import jax, jax.numpy as jnp
        import numpy as np
        C, H, W_IMG = (3, 224, 224)
        NP = 14
        PS = H // NP
        D_IN = C * PS * PS
        D = 192
        SEQ = NP * NP + 1
        B = 128

        def _sinusoidal_pos_embed(seq_len, d):
            i = np.arange(seq_len, dtype=np.float64)[:, None]
            j = np.arange(d, dtype=np.float64)[None, :]
            angle = i / np.power(10000.0, (j - j % 2) / d)
            pe = np.where(j % 2 == 0, np.sin(angle), np.cos(angle))
            return jnp.asarray(pe, dtype=jnp.float32)
        key = jax.random.key(seed)
        kx, kw, kc = jax.random.split(key, 3)
        x = jax.random.normal(kx, (B, C, H, W_IMG), dtype=jnp.float32)
        W = jax.random.normal(kw, (D, D_IN), dtype=jnp.float32) * 0.02
        b = jnp.zeros((D,), dtype=jnp.float32)
        class_token = jax.random.uniform(kc, (1, D), dtype=jnp.float32)
        pos_embed = _sinusoidal_pos_embed(SEQ, D)
        return {'x': x, 'W': W, 'b': b, 'class_token': class_token, 'pos_embed': pos_embed}
    _L0_tok_all = _L0_tok_setup()
    _L0_tok_in = {k: v for k, v in _L0_tok_all.items() if k in ('W', 'b', 'class_token', 'pos_embed')}
    del _L0_tok_all

    def _L0_attn_setup():
        import jax, jax.numpy as jnp
        import numpy as np
        HALF_WIN = 6

        def _local_attn(x, w_qkv, w_proj, b_proj, num_heads=12):
            B, N, C = x.shape
            H = num_heads
            D = C // H
            W = 2 * HALF_WIN + 1
            qkv = (x @ w_qkv).reshape(B, N, 3, H, D)
            q, k, v = (qkv[:, :, 0], qkv[:, :, 1], qkv[:, :, 2])
            offs = jnp.arange(-HALF_WIN, HALF_WIN + 1)
            idx = jnp.arange(N)[:, None] + offs[None, :]
            valid = (idx >= 0) & (idx < N)
            idxc = jnp.clip(idx, 0, N - 1)
            k_win = k[:, idxc]
            v_win = v[:, idxc]
            scale = D ** (-0.5)
            scores = jnp.einsum('bnhd,bnwhd->bnhw', q, k_win) * scale
            neg = jnp.asarray(jnp.finfo(scores.dtype).min, scores.dtype)
            scores = jnp.where(valid[None, :, None, :], scores, neg)
            p = jax.nn.softmax(scores, axis=-1)
            out = jnp.einsum('bnhw,bnwhd->bnhd', p, v_win)
            out = out.reshape(B, N, C)
            return out @ w_proj + b_proj
        key = jax.random.key(seed)
        k1, k2, k3 = jax.random.split(key, 3)
        B, N, C = (2, 1024, 192)
        x = jax.random.normal(k1, (B, N, C), dtype=jnp.float32)
        s = 1.0 / np.sqrt(C)
        w_qkv = jax.random.uniform(k2, (C, 3 * C), jnp.float32, -s, s)
        w_proj = jax.random.uniform(k3, (C, C), jnp.float32, -s, s)
        b_proj = jnp.zeros((C,), jnp.float32)
        return {'x': x, 'w_qkv': w_qkv, 'w_proj': w_proj, 'b_proj': b_proj}
    _L0_attn_all = _L0_attn_setup()
    _L0_attn_in = {k: v for k, v in _L0_attn_all.items() if k in ('w_qkv', 'w_proj', 'b_proj')}
    del _L0_attn_all

    def _L0_ffn_setup():
        import jax, jax.numpy as jnp
        import numpy as np
        E, C, F, K = (8, 192, 768, 2)
        key = jax.random.key(seed)
        k0, k1, k2, k3 = jax.random.split(key, 4)
        B, T = (8, 512)
        return {'x': jax.random.normal(k0, (B, T, C), jnp.float32), 'router_w': jax.random.normal(k1, (E, C), jnp.float32) * 0.02, 'w1': jax.random.normal(k2, (E, C, F), jnp.float32) * 0.02, 'b1': jnp.zeros((E, F), jnp.float32), 'w2': jax.random.normal(k3, (E, F, C), jnp.float32) * 0.02, 'b2': jnp.zeros((E, C), jnp.float32)}
    _L0_ffn_all = _L0_ffn_setup()
    _L0_ffn_in = {k: v for k, v in _L0_ffn_all.items() if k in ('router_w', 'w1', 'b1', 'w2', 'b2')}
    del _L0_ffn_all
    return {'x': x, 'L0_tok_W': _L0_tok_in['W'], 'L0_tok_b': _L0_tok_in['b'], 'L0_tok_class_token': _L0_tok_in['class_token'], 'L0_tok_pos_embed': _L0_tok_in['pos_embed'], 'L0_attn_w_qkv': _L0_attn_in['w_qkv'], 'L0_attn_w_proj': _L0_attn_in['w_proj'], 'L0_attn_b_proj': _L0_attn_in['b_proj'], 'L0_ffn_router_w': _L0_ffn_in['router_w'], 'L0_ffn_w1': _L0_ffn_in['w1'], 'L0_ffn_b1': _L0_ffn_in['b1'], 'L0_ffn_w2': _L0_ffn_in['w2'], 'L0_ffn_b2': _L0_ffn_in['b2']}

def reference(x, L0_tok_W, L0_tok_b, L0_tok_class_token, L0_tok_pos_embed, L0_attn_w_qkv, L0_attn_w_proj, L0_attn_b_proj, L0_ffn_router_w, L0_ffn_w1, L0_ffn_b1, L0_ffn_w2, L0_ffn_b2):
    import jax
    import jax.numpy as jnp

    def _L0_tok_ref(x, W, b, class_token, pos_embed):
        import jax, jax.numpy as jnp
        import numpy as np
        C, H, W_IMG = (3, 224, 224)
        NP = 14
        PS = H // NP
        D_IN = C * PS * PS
        D = 192
        SEQ = NP * NP + 1
        B = 128

        def _sinusoidal_pos_embed(seq_len, d):
            i = np.arange(seq_len, dtype=np.float64)[:, None]
            j = np.arange(d, dtype=np.float64)[None, :]
            angle = i / np.power(10000.0, (j - j % 2) / d)
            pe = np.where(j % 2 == 0, np.sin(angle), np.cos(angle))
            return jnp.asarray(pe, dtype=jnp.float32)
        n = x.shape[0]
        p = x.reshape(n, C, NP, PS, NP, PS)
        p = p.transpose(0, 2, 4, 1, 3, 5).reshape(n, NP * NP, D_IN)
        tokens = jnp.einsum('npd,hd->nph', p, W) + b
        cls = jnp.broadcast_to(class_token[None], (n, 1, D))
        tokens = jnp.concatenate([cls, tokens], axis=1)
        return tokens + pos_embed[None]

    def _L0_attn_ref(x, w_qkv, w_proj, b_proj):
        import jax, jax.numpy as jnp
        import numpy as np
        HALF_WIN = 6

        def _local_attn(x, w_qkv, w_proj, b_proj, num_heads=12):
            B, N, C = x.shape
            H = num_heads
            D = C // H
            W = 2 * HALF_WIN + 1
            qkv = (x @ w_qkv).reshape(B, N, 3, H, D)
            q, k, v = (qkv[:, :, 0], qkv[:, :, 1], qkv[:, :, 2])
            offs = jnp.arange(-HALF_WIN, HALF_WIN + 1)
            idx = jnp.arange(N)[:, None] + offs[None, :]
            valid = (idx >= 0) & (idx < N)
            idxc = jnp.clip(idx, 0, N - 1)
            k_win = k[:, idxc]
            v_win = v[:, idxc]
            scale = D ** (-0.5)
            scores = jnp.einsum('bnhd,bnwhd->bnhw', q, k_win) * scale
            neg = jnp.asarray(jnp.finfo(scores.dtype).min, scores.dtype)
            scores = jnp.where(valid[None, :, None, :], scores, neg)
            p = jax.nn.softmax(scores, axis=-1)
            out = jnp.einsum('bnhw,bnwhd->bnhd', p, v_win)
            out = out.reshape(B, N, C)
            return out @ w_proj + b_proj
        return _local_attn(x, w_qkv, w_proj, b_proj)

    def _L0_ffn_ref(x, router_w, w1, b1, w2, b2):
        import jax, jax.numpy as jnp
        import numpy as np
        E, C, F, K = (8, 192, 768, 2)
        B, T, Cc = x.shape
        flat = x.reshape(-1, Cc)
        logits = flat @ router_w.T
        probs = jax.nn.softmax(logits.astype(jnp.float32), axis=-1)
        top_w, top_i = jax.lax.top_k(probs, K)
        top_w = (top_w / top_w.sum(-1, keepdims=True)).astype(x.dtype)
        out = jnp.zeros_like(flat)
        for e in range(E):
            w_e = jnp.sum(top_w * (top_i == e), axis=-1)[:, None]
            h = jax.nn.gelu(flat @ w1[e] + b1[e], approximate=False)
            out = out + w_e * (h @ w2[e] + b2[e])
        return out.reshape(B, T, Cc)
    h = _L0_tok_ref(x, L0_tok_W, L0_tok_b, L0_tok_class_token, L0_tok_pos_embed)
    h = h + _L0_attn_ref(_layernorm(h, axis=-1), L0_attn_w_qkv, L0_attn_w_proj, L0_attn_b_proj)
    h = h + _L0_ffn_ref(_layernorm(h, axis=-1), L0_ffn_router_w, L0_ffn_w1, L0_ffn_b1, L0_ffn_w2, L0_ffn_b2)
    return h

_drawn_inputs = setup_inputs


def setup_inputs(seed=0):
    import zlib

    import numpy as np

    out = dict(_drawn_inputs(seed))
    spreads = {'L0_tok_b': (0.0, 0.1),
     'L0_attn_b_proj': (0.0, 0.1),
     'L0_ffn_b1': (0.0, 0.358),
     'L0_ffn_b2': (0.0, 0.1)}
    factors = {}
    for name, (base, spread) in spreads.items():
        noise = np.random.default_rng([zlib.crc32(name.encode()), seed]).standard_normal(out[name].shape)
        drawn = base * np.exp(spread * noise) if base else spread * noise
        out[name] = jnp.asarray(drawn.astype(out[name].dtype))
    for name, factor in factors.items():
        out[name] = (out[name] * factor).astype(out[name].dtype)
    return out
```

```python
from contextlib import ExitStack

import numpy as np

import concourse.bass as bass
from concourse import mybir

F32 = mybir.dt.float32
F16 = mybir.dt.float16
BF16 = mybir.dt.bfloat16
ALU = mybir.AluOpType
ACT = mybir.ActivationFunctionType
AX = mybir.AxisListType

IMGS, CHANS, SIDE, NPATCH = 64, 3, 224, 14
PATCH = SIDE // NPATCH
SEQ = NPATCH * NPATCH + 1
D = 192
DIN = CHANS * PATCH * PATCH
KIN = DIN // 128
HEADS, DH = 12, 16
GROUPS = 3
HPG = HEADS // GROUPS
HALF_WIN = 6
ROWS = (SEQ + 1) // 2
PITCH = ROWS + ROWS % 2
TILE_AT = (0, SEQ - ROWS)
KEYS = ROWS + HALF_WIN
KEYS_AT = (0, SEQ - KEYS)
EXPERTS, FF = 8, 768
MF = FF // 128
WS = 64.0
EPS = 1e-5
MASKED = -1e30
TOKENS = IMGS * SEQ
SUPER = 3
NSUP = SUPER * 128
SUPERS = -(-TOKENS // NSUP)
TILES = SUPERS * SUPER
PAD_TOKENS = TILES * 128

STACK = [list(range(128)), list(range(128, 192)) + list(range(64)), list(range(64, 192))]
PRODUCTS = [(0, 0, 0), (1, 1, 0), (2, 2, 0), (0, 0, 1), (1, 1, 1)]


def need(eng, sem, value):
    if not isinstance(value, int) or value > 0:
        eng.wait_ge(sem, value)


def need_apart(eng, sem, value, met):
    eng.wait_ge(*met)
    eng.wait_ge(sem, value)


def pipeline(eng, body):
    for t in range(4):
        body(t, t)
    with eng.Fori(1, IMGS // 4) as p:
        for k in range(4):
            body(4 * p + k, k)
    for t in (IMGS, IMGS + 1):
        body(t, t % 4)


def runs(t):
    if isinstance(t, int):
        return t < IMGS, 1 <= t <= IMGS, t >= 2
    return True, True, True


def vit_tower(nc, xt, w_embed, bias_tab, pos, w_qk, w_v, w_p, b_p, router, w1, b1, w2, b2,
              ident, band, low_rows, out):
    h2_dram = nc.dram_tensor("h2_scratch", (PAD_TOKENS, D), F32).ap()
    xs2_dram = nc.dram_tensor("xs2_scratch", (PAD_TOKENS, 2 * D), F16).ap()
    attention_part(nc, xt, w_embed, bias_tab, pos, w_qk, w_v, w_p, b_p, ident, band, low_rows,
                   h2_dram, xs2_dram)
    experts_part(nc, router, w1, b1, w2, b2, ident, h2_dram, xs2_dram, out)


def attention_part(nc, xt, w_embed, bias_tab, pos, w_qk, w_v, w_p, b_p, ident, band, low_rows,
                   h2_dram, xs2_dram):
    with ExitStack() as ctx:
        def sb(name, shape, dt):
            return ctx.enter_context(nc.sbuf_tensor(name, shape, dt))

        def pb(name, shape, dt):
            return ctx.enter_context(nc.psum_tensor(name, shape, dt))

        def sem(name):
            return ctx.enter_context(nc.semaphore(name))

        identf = sb("identf", [128, 128], F32)
        ident16 = sb("ident16", [128, 128], F16)
        identb = sb("identb", [128, 128], BF16)
        bandf = sb("bandf", [ROWS, 2, KEYS], F32)
        bandb = sb("bandb", [ROWS, 2, KEYS], BF16)
        low = sb("low", [128, 1], F32)
        we = sb("we", [128, KIN, D], F32)
        tab = sb("tab", [ROWS, 2, D], F32)
        post = sb("post", [ROWS, 2, D], F32)
        wqk32 = sb("wqk32", [128, 3, 2 * GROUPS * 128], F32)
        wqk = [sb("wqk_hi", [128, 3, 2 * GROUPS * 128], F16), sb("wqk_lo", [128, 2, 2 * GROUPS * 128], F16)]
        wv32 = sb("wv32", [128, 3, D], F32)
        wv = [sb("wv_hi", [128, 3, D], F16), sb("wv_lo", [128, 2, D], F16)]
        wp32 = sb("wp32", [128, 3, D], F32)
        wp = [sb("wp_hi", [128, 3, D], F16), sb("wp_lo", [128, 2, D], F16)]
        bp32 = sb("bp32", [64, D], F32)
        bp = sb("bp", [128, D], F16)
        two_rows = sb("two_rows", [128, 128], F16)
        zero_row = sb("zero_row", [64, D], F32)
        half_pow = sb("half_pow", [128, 2], F32)
        eps = sb("eps", [128, 2], F32)

        patches = [sb(f"patches{k}", [128, KIN, SEQ], F32) for k in range(2)]
        h1 = [sb(f"h1_{k}", [ROWS, 2, D], F32) for k in range(4)]
        st1 = sb("st1", [ROWS, 2, 6], F32)
        mv1 = sb("mv1", [ROWS, 2, 2], F32)
        rs1 = sb("rs1", [ROWS, 2], F32)
        xn1 = sb("xn1", [ROWS, 2, D], F32)
        xs1 = sb("xs1", [ROWS, 2, 2 * D], F16)
        xT1 = sb("xT1", [128, 3, SEQ], F16)
        qk_hi = sb("qk_hi", [128, GROUPS, 2, SEQ], F16)
        q_lo = sb("q_lo", [128, GROUPS, SEQ], F16)
        k_st = sb("k_st", [128, GROUPS, SEQ], F16)
        k_diag = sb("k_diag", [128, GROUPS, HPG, SEQ], F16)

        v_hi = sb("v_hi", [KEYS, 2, HEADS, DH + 1], F16)
        v_lo = sb("v_lo", [KEYS, 2, HEADS, DH + 1], F16)
        mx = [sb(f"mx{k}", [ROWS, GROUPS, HPG], F32) for k in range(2)]
        prob = [sb(f"prob{k}", [ROWS, GROUPS, HPG, KEYS], F32) for k in range(2)]
        pT_hi = [sb(f"pT_hi{k}", [KEYS, GROUPS, HPG * ROWS], F16) for k in range(2)]
        pT_lo = [sb(f"pT_lo{k}", [KEYS, GROUPS, HPG * ROWS], F16) for k in range(2)]
        rden = sb("rden", [ROWS, 2, HEADS], F32)
        on = sb("on", [ROWS, 2, D], F32)
        os_ = sb("os", [ROWS, 2, 2 * D], F16)

        oT = sb("oT", [128, 2, 3, ROWS], F16)
        h2 = [sb(f"h2_{k}", [ROWS, 2, D], F32) for k in range(2)]
        st2 = sb("st2", [ROWS, 2, 6], F32)
        mv2 = sb("mv2", [ROWS, 2, 2], F32)
        rs2 = sb("rs2", [ROWS, 2], F32)
        xn2 = sb("xn2", [ROWS, 2, D], F32)
        xs2 = [sb(f"xs2_{k}", [ROWS, 2, 2 * D], F16) for k in range(2)]

        big = [pb(f"big{k}", [128, 3, 512], F32) for k in range(2)]
        small = [pb(f"small{k}", [128, 512], F32) for k in range(2)]

        names = ("load_c zero_mem zeros_out weights embedded h1_set stats1 aggr1 rstd1 normed1 hi1 lo1 turned1 xT_set qk_done "
                 "qk_hi_set q_lo_set k_st_set k_diag_set v_done v_hi_set v_lo_set norm_done o_hi_set "
                 "o_lo_set o_turned oT_set proj_done h2_set stats2 aggr2 rstd2 normed2 hi2 lo2 den_set "
                 "pv_done var1 var2 setup1 setup2").split()
        s = {n: sem(n) for n in names}
        s_max, s_score, s_sub, s_exp, s_pT, s_phi, s_plo = (
            [sem(f"{n}{k}") for k in range(2)]
            for n in ("max_set", "scored", "shifted", "exp_set", "prob_turned", "p_hi_set", "p_lo_set"))
        s_patch = [sem(f"patches_in{k}") for k in range(2)]
        s_h2out = [sem(f"h2_out{k}") for k in range(2)]
        s_xsout = [sem(f"xs2_out{k}") for k in range(2)]
        LOADS = 12

        block = ctx.enter_context(nc.Block())

        @block.sync
        def _(sp):
            for dst, src in ((we[:], w_embed), (tab[:], bias_tab), (post[:], pos), (identf[:], ident), (bandf[:], band),
                             (low[:], low_rows), (wqk32[:], w_qk), (wv32[:], w_v), (wp32[:], w_p)):
                sp.dma_start(dst, src).then_inc(s["load_c"], 16)
            sp.wait_ge(s["zero_mem"], 1)
            for row in (0, 32):
                sp.dma_start(bp32[row:row + 1, :], b_p).then_inc(s["load_c"], 16)
            sp.wait_ge(s["load_c"], 16 * (LOADS - 1))
            for at in range(TOKENS, PAD_TOKENS, 64):
                n = min(64, PAD_TOKENS - at)
                sp.dma_start(h2_dram[at:at + n, :], zero_row[0:n, :]).then_inc(s["zeros_out"], 16)
                sp.dma_start(xs2_dram[at:at + n, :], zero_row[0:n, :].bitcast(F16)).then_inc(s["zeros_out"], 16)

            def body(t, k):
                front, attention, back = runs(t)
                if front:
                    need(sp, s["embedded"], t - 1)
                    src = xt[t:t + 1] if isinstance(t, int) else xt[bass.ds(t, 1)]
                    sp.dma_start(patches[k % 2][:], src.rearrange("a p k n -> p (a k) n")).then_inc(s_patch[k % 2], 16)

            pipeline(sp, body)

        @block.gpsimd
        def _(pool):
            pool.memset(bp32[:], 0.0)
            pool.memset(zero_row[:], 0.0)
            pool.memset(bp[:], 0.0)
            pool.memset(two_rows[:], 0.0)
            pool.memset(half_pow[:], -0.5)
            pool.memset(eps[:], EPS)
            pool.memset(v_hi[:], WS)
            pool.memset(v_lo[:], 0.0)
            pool.memset(k_diag[:], 0.0).then_inc(s["zero_mem"], 1)
            pool.wait_ge(s["zero_mem"], 1)
            for n, row in enumerate((0, 32)):
                pool.memset(two_rows[row:row + 1, :], 1.0).then_inc(s["setup1"], 1)
                pool.wait_ge(s["setup1"], n + 1)

            def body(t, k):
                front, attention, back = runs(t)
                f, b = t, t - 2
                if front:
                    pool.wait_ge(s["aggr1"], f + 1)
                    pool.tensor_tensor(mv1[:, :, 1], mv1[:, :, 1], eps[0:ROWS, :], ALU.add).then_inc(s["var1"], 1)
                    pool.wait_ge(s["var1"], f + 1)
                    need(pool, s["normed1"], f)
                    pool.tensor_tensor(rs1[:], mv1[:, :, 1], half_pow[0:ROWS, :], ALU.pow).then_inc(s["rstd1"], 1)
                    pool.wait_ge(s["hi1"], f + 1)
                    need(pool, s["turned1"], f)
                    pool.tensor_tensor(xs1[:, :, D:], xn1[:], xs1[:, :, 0:D], ALU.subtract).then_inc(s["lo1"], 1)
                if back:
                    pool.wait_ge(s["aggr2"], b + 1)
                    pool.tensor_tensor(mv2[:, :, 1], mv2[:, :, 1], eps[0:ROWS, :], ALU.add).then_inc(s["var2"], 1)
                    pool.wait_ge(s["var2"], b + 1)
                    need(pool, s["normed2"], b)
                    pool.tensor_tensor(rs2[:], mv2[:, :, 1], half_pow[0:ROWS, :], ALU.pow).then_inc(s["rstd2"], 1)
                    pool.wait_ge(s["hi2"], b + 1)
                    pool.tensor_tensor(xs2[k % 2][:, :, D:], xn2[:], xs2[k % 2][:, :, 0:D], ALU.subtract)\
                        .then_inc(s["lo2"], 1)
                if attention:
                    a = t - 1
                    pool.wait_ge(s["o_hi_set"], a + 1)
                    pool.tensor_tensor(os_[:, :, D:], on[:], os_[:, :, 0:D], ALU.subtract).then_inc(s["o_lo_set"], 1)

            pipeline(pool, body)

        @block.scalar
        def _(act):
            act.wait_ge(s["load_c"], 16 * (LOADS - 1))
            act.copy(ident16[:], identf[:])
            act.copy(identb[:], identf[:])
            act.copy(bandb[:], bandf[:]).then_inc(s["setup2"], 1)
            for hi, w in ((wqk[0], wqk32), (wv[0], wv32), (wp[0], wp32)):
                act.mul(hi[:], w[:], WS).then_inc(s["weights"], 1)
            act.wait_ge(s["setup1"], 2)
            for row in (0, 32):
                act.mul(bp[row:row + 1, :], bp32[row:row + 1, :], WS).then_inc(s["weights"], 1)

            def body(t, k):
                front, attention, back = runs(t)
                f, a, b = t, t - 1, t - 2
                if attention:
                    for n in range(2):
                        act.wait_ge(s_sub[n], a + 1)
                        act.activation(prob[n][:], prob[n][:], ACT.Exp, scale=DH ** -0.5 / (WS * WS)).then_inc(s_exp[n], 1)
                if back:
                    act.wait_ge(s["o_turned"], b + 1)
                    need(act, s["proj_done"], b)
                    act.copy(oT[:].rearrange("p n c r -> p (n c) r"),
                             small[1][:].bitcast(F16)[:, 0:6 * PITCH].rearrange("p (m r) -> p m r", m=6)[:, :, 0:ROWS]).then_inc(s["oT_set"], 1)
                if attention:
                    act.wait_ge(s["v_done"], a + 1)
                    need(act, s["pv_done"], a)
                    act.copy(v_hi[:, :, :, 0:DH], small[0][0:KEYS, 0:2 * D].rearrange("p (n h d) -> p n h d", n=2, h=HEADS))\
                        .then_inc(s["v_hi_set"], 1)
                if front:
                    act.wait_ge(s["normed1"], f + 1)
                    need(act, s["turned1"], f)
                    act.copy(xs1[:, :, 0:D], xn1[:]).then_inc(s["hi1"], 1)
                if attention:
                    for n in range(2):
                        act.wait_ge(s_pT[n], a + 1)
                        need(act, s["pv_done"], a)
                        act.copy(pT_hi[n][:], big[n][0:KEYS, :, 0:HPG * ROWS]).then_inc(s_phi[n], 1)
                if back:
                    act.wait_ge(s["normed2"], b + 1)
                    need(act, s_xsout[k % 2], 16 * (b - k % 2))
                    act.copy(xs2[k % 2][:, :, 0:D], xn2[:]).then_inc(s["hi2"], 1)
                if front:
                    act.wait_ge(s["qk_done"], f + 1)
                    need(act, s_score[1], f)
                    act.copy(qk_hi[:].rearrange("p g w n -> p g (w n)"), big[0][:, :, 0:2 * SEQ]).then_inc(s["qk_hi_set"], 1)
                if attention:
                    act.wait_ge(s["norm_done"], a + 1)
                    need(act, s["o_turned"], a)
                    act.copy(os_[:, :, 0:D], on[:]).then_inc(s["o_hi_set"], 1)
                if back:
                    act.wait_ge(s["h2_set"], b + 1)
                    act.wait_ge(s["lo2"], b + 1)
                    for src, dst, done in ((h2[k % 2], h2_dram, s_h2out[k % 2]), (xs2[k % 2], xs2_dram, s_xsout[k % 2])):
                        for n, lead in ((0, 0), (1, 1)):
                            rows = ROWS - lead
                            at = b * SEQ + (TILE_AT[1] + 1) * n
                            d = dst[at:at + rows, :] if isinstance(at, int) else dst[bass.ds(at, rows), :]
                            act.dma_start(d, src[lead:ROWS, n, :]).then_inc(done, 16)

            pipeline(act, body)
            for k in range(2):
                act.wait_ge(s_h2out[k], 16 * IMGS)
                act.wait_ge(s_xsout[k], 16 * IMGS)
            act.wait_ge(s["zeros_out"], 32 * -(-(PAD_TOKENS - TOKENS) // 64))

        @block.vector
        def _(dve):
            dve.wait_ge(s["load_c"], 16 * (LOADS - 1))
            dve.tensor_tensor(tab[:], tab[:], post[:], ALU.add)
            for n, (pair, w) in enumerate(((wqk, wqk32), (wv, wv32), (wp, wp32))):
                dve.wait_ge(s["weights"], n + 1)
                dve.scalar_tensor_tensor(out=pair[1][:], in0=w[:, 0:2, :], scalar=WS, in1=pair[0][:, 0:2, :],
                                         op0=ALU.mult, op1=ALU.subtract)
            dve.wait_ge(s["weights"], 5)
            dve.scalar_tensor_tensor(out=bp[32:33, :], in0=bp32[32:33, :], scalar=WS, in1=bp[32:33, :],
                                     op0=ALU.mult, op1=ALU.subtract).then_inc(s["setup2"], 1)

            def normalise(mv, rs, xn, h):
                for n in range(2):
                    ins = dve.tensor_scalar(xn[:, n, :], h[:, n, :], mv[:, n, 0:1], rs[:, n:n + 1], ALU.subtract, ALU.mult)
                return ins

            def statistics(h, st, mv, stats, aggr, n_th):
                for n in range(2):
                    ins = dve.bn_stats(st[:, n, :], h[:, n, :])
                ins.then_inc(stats, 1)
                need_apart(dve, stats, n_th, (s["load_c"], 16))
                for n in range(2):
                    ins = dve.bn_aggr(mv[:, n, :], st[:, n, :])
                ins.then_inc(aggr, 1)

            def body(t, k):
                front, attention, back = runs(t)
                f, a, b = t, t - 1, t - 2
                if front:
                    dve.wait_ge(s["embedded"], f + 1)
                    dve.tensor_tensor(h1[k][:], small[0][0:ROWS, 0:2 * D].rearrange("p (n c) -> p n c", n=2), tab[:],
                                      ALU.add).then_inc(s["h1_set"], 1)
                    dve.wait_ge(s["h1_set"], f + 1)
                    need(dve, s["rstd1"], f)
                    statistics(h1[k], st1, mv1, s["stats1"], s["aggr1"], f + 1)
                if attention:
                    for n in range(2):
                        scores = big[n][0:ROWS, :, 0:HPG * KEYS].rearrange("p g (h c) -> p g h c", h=HPG)
                        dve.wait_ge(s_score[n], a + 1)
                        dve.tensor_reduce(mx[n][:], scores, AX.X, ALU.max).then_inc(s_max[n], 1)
                        dve.wait_ge(s_max[n], a + 1)
                        need(dve, s_pT[n], a)
                        dve.tensor_tensor(prob[n][:], scores, mx[n][:].unsqueeze(3).to_broadcast([ROWS, GROUPS, HPG, KEYS]),
                                          ALU.subtract).then_inc(s_sub[n], 1)
                    dve.wait_ge(s["v_hi_set"], a + 1)
                    need(dve, s["pv_done"], a)
                    dve.tensor_tensor(v_lo[:, :, :, 0:DH], small[0][0:KEYS, 0:2 * D].rearrange("p (n h d) -> p n h d", n=2, h=HEADS),
                                      v_hi[:, :, :, 0:DH], ALU.subtract).then_inc(s["v_lo_set"], 1)
                if front:
                    dve.wait_ge(s["rstd1"], f + 1)
                    need(dve, s["lo1"], f)
                    normalise(mv1, rs1, xn1, h1[k]).then_inc(s["normed1"], 1)
                if back:
                    dve.wait_ge(s["proj_done"], b + 1)
                    need(dve, s_h2out[k % 2], 16 * (b - k % 2))
                    dve.scalar_tensor_tensor(out=h2[k % 2][:].rearrange("p n c -> p (n c)"), in0=small[1][0:ROWS, 0:2 * D], scalar=1.0 / WS,
                                             in1=h1[(k + 2) % 4][:].rearrange("p n c -> p (n c)"), op0=ALU.mult, op1=ALU.add).then_inc(s["h2_set"], 1)
                    dve.wait_ge(s["h2_set"], b + 1)
                    need(dve, s["rstd2"], b)
                    statistics(h2[k % 2], st2, mv2, s["stats2"], s["aggr2"], b + 1)
                if attention:
                    for n in range(2):
                        dve.wait_ge(s_phi[n], a + 1)
                        need(dve, s["pv_done"], a)
                        dve.tensor_tensor(pT_lo[n][:], big[n][0:KEYS, :, 0:HPG * ROWS], pT_hi[n][:], ALU.subtract)\
                            .then_inc(s_plo[n], 1)
                if back:
                    dve.wait_ge(s["rstd2"], b + 1)
                    need(dve, s["lo2"], b)
                    normalise(mv2, rs2, xn2, h2[k % 2]).then_inc(s["normed2"], 1)
                if front:
                    dve.wait_ge(s["turned1"], f + 1)
                    need(dve, s["v_done"], f)
                    for n in range(2):
                        ins = dve.tensor_copy(xT1[:, :, TILE_AT[n] + n:TILE_AT[n] + ROWS],
                                              small[0][:].bitcast(F16)[:, 0:6 * PITCH].rearrange("p (n c r) -> p n c r", n=2, c=3)[:, n, :, n:ROWS])
                    ins.then_inc(s["xT_set"], 1)
                    dve.wait_ge(s["qk_hi_set"], f + 1)
                    need(dve, s_score[1], f)
                    dve.tensor_tensor(q_lo[:], big[0][:, :, 0:SEQ], qk_hi[:, :, 0, :], ALU.subtract).then_inc(s["q_lo_set"], 1)
                    dve.scalar_tensor_tensor(out=k_st[:], in0=qk_hi[:, :, 1, :], scalar=low[:, 0:1],
                                             in1=big[0][:, :, SEQ:2 * SEQ], op0=ALU.mult, op1=ALU.add).then_inc(s["k_st_set"], 1)
                    dve.wait_ge(s["k_st_set"], f + 1)
                    for h in range(HPG):
                        q = slice(32 * h, 32 * h + 32)
                        ins = dve.tensor_copy(k_diag[q, :, h, :], k_st[q, :, :])
                    ins.then_inc(s["k_diag_set"], 1)
                if attention:
                    dve.wait_ge(s["pv_done"], a + 1)
                    o = small[1][0:ROWS, 0:2 * HEADS * (DH + 1)].rearrange("p (n h d) -> p n h d", n=2, h=HEADS)
                    dve.reciprocal(rden[:], o[:, :, :, DH]).then_inc(s["den_set"], 1)
                    dve.wait_ge(s["den_set"], a + 1)
                    need(dve, s["o_lo_set"], a)
                    dve.tensor_tensor(on[:].rearrange("p n (h d) -> p n h d", h=HEADS), o[:, :, :, 0:DH],
                                      rden[:].unsqueeze(3).to_broadcast([ROWS, 2, HEADS, DH]), ALU.mult).then_inc(s["norm_done"], 1)

            pipeline(dve, body)

        @block.tensor
        def _(pe):
            pe.wait_ge(s["setup1"], 2)
            pe.wait_ge(s["setup2"], 2)

            def turn(src, dst):
                for n in range(2):
                    for c in range(3):
                        at = (3 * n + c) * PITCH
                        ins = pe.transpose(dst[:, at:at + ROWS], src[:, n, 128 * c:128 * c + 128], ident16[0:ROWS, 0:ROWS])
                return ins

            def body(t, k):
                front, attention, back = runs(t)
                f, a, b = t, t - 1, t - 2
                if front:
                    pe.wait_ge(s_patch[k % 2], 16 + 8 * (f - k % 2))
                    need(pe, s["xT_set"], f)
                    for n in range(2):
                        for c in range(KIN):
                            ins = pe.matmul(small[0][0:ROWS, n * D:n * D + D], patches[k % 2][:, c, TILE_AT[n]:TILE_AT[n] + ROWS],
                                            we[:, c, :], start=(c == 0), stop=(c == KIN - 1))
                    ins.then_inc(s["embedded"], 1)
                if attention:
                    pe.wait_ge(s["k_diag_set"], a + 1)
                    pe.wait_ge(s["q_lo_set"], a + 1)
                    for n in range(2):
                        need(pe, s_plo[n], a)
                        rows = slice(TILE_AT[n], TILE_AT[n] + ROWS)
                        for g in range(GROUPS):
                            dst = big[n][0:ROWS, g, 0:HPG * KEYS]
                            keys = k_diag[:, g, :, KEYS_AT[n]:KEYS_AT[n] + KEYS]
                            pe.matmul(dst, identb[0:ROWS, 0:ROWS],
                                      bandb[:, n, :].unsqueeze(1).to_broadcast([ROWS, HPG, KEYS]), start=True, stop=False)
                            pe.matmul(dst, qk_hi[:, g, 0, rows], keys, start=False, stop=False)
                            ins = pe.matmul(dst, q_lo[:, g, rows], keys, start=False, stop=True)
                        ins.then_inc(s_score[n], 1)
                if back:
                    pe.wait_ge(s["o_lo_set"], b + 1)
                    turn(os_, small[1][:].bitcast(F16)).then_inc(s["o_turned"], 1)
                if attention:
                    if front:
                        pe.wait_ge(s["h1_set"], f + 1)
                    for n in range(2):
                        for j, (c, w, half) in enumerate(PRODUCTS):
                            ins = pe.matmul(small[0][0:KEYS, n * D:n * D + D], xT1[:, c, KEYS_AT[n]:KEYS_AT[n] + KEYS],
                                            wv[half][:, w, :], start=(j == 0), stop=(j == len(PRODUCTS) - 1))
                    ins.then_inc(s["v_done"], 1)
                if back:
                    pe.wait_ge(s["oT_set"], b + 1)
                    for n in range(2):
                        dst = small[1][0:ROWS, n * D:n * D + D]
                        pe.matmul(dst, two_rows[:, 0:ROWS], bp[:], start=True, stop=False)
                        for j, (c, w, half) in enumerate(PRODUCTS):
                            ins = pe.matmul(dst, oT[:, n, c, :], wp[half][:, w, :], start=False, stop=(j == len(PRODUCTS) - 1))
                    ins.then_inc(s["proj_done"], 1)
                if attention:
                    for n in range(2):
                        pe.wait_ge(s_exp[n], a + 1)
                        for g in range(GROUPS):
                            for h in range(HPG):
                                ins = pe.transpose(big[n][0:KEYS, g, h * ROWS:h * ROWS + ROWS], prob[n][:, g, h, :],
                                                   identf[0:ROWS, 0:ROWS])
                        ins.then_inc(s_pT[n], 1)
                if front:
                    pe.wait_ge(s["lo1"], f + 1)
                    if attention:
                        pe.wait_ge(s["v_lo_set"], a + 1)
                    else:
                        pe.wait_ge(s["h1_set"], f + 1)
                    turn(xs1, small[0][:].bitcast(F16)).then_inc(s["turned1"], 1)
                    pe.wait_ge(s["xT_set"], f + 1)
                    if attention:
                        pe.wait_ge(s_plo[0], a + 1)
                    for g in range(GROUPS):
                        for which in range(2):
                            for j, (c, w, half) in enumerate(PRODUCTS):
                                col = (which * GROUPS + g) * 128
                                ins = pe.matmul(big[0][:, g, which * SEQ:(which + 1) * SEQ], wqk[half][:, w, col:col + 128],
                                                xT1[:, c, :], start=(j == 0), stop=(j == len(PRODUCTS) - 1))
                    ins.then_inc(s["qk_done"], 1)
                if attention:
                    if back:
                        pe.wait_ge(s["h2_set"], b + 1)
                    need(pe, s["v_lo_set"], a + 1)
                    for n in range(2):
                        pe.wait_ge(s_plo[n], a + 1)
                        for h in range(HEADS):
                            g, cols = h // HPG, slice((h % HPG) * ROWS, (h % HPG + 1) * ROWS)
                            at = (n * HEADS + h) * (DH + 1)
                            dst = small[1][0:ROWS, at:at + DH + 1]
                            pe.matmul(dst, pT_hi[n][:, g, cols], v_hi[:, n, h, :], start=True, stop=False)
                            pe.matmul(dst, pT_hi[n][:, g, cols], v_lo[:, n, h, :], start=False, stop=False)
                            ins = pe.matmul(dst, pT_lo[n][:, g, cols], v_hi[:, n, h, :], start=False, stop=True)
                    ins.then_inc(s["pv_done"], 1)

            pipeline(pe, body)


def super_pipeline(eng, body):
    body(0, 0)
    with eng.Fori(0, (SUPERS - 3) // 2) as p:
        for k in (1, 2):
            body(2 * p + k, k % 2)
    for st in (SUPERS - 2, SUPERS - 1):
        body(st, st % 2)


def experts_part(nc, router, w1, b1, w2, b2, ident, h2_dram, xs2_dram, out):
    with ExitStack() as ctx:
        def sb(name, shape, dt):
            return ctx.enter_context(nc.sbuf_tensor(name, shape, dt))

        def pb(name, shape, dt):
            return ctx.enter_context(nc.psum_tensor(name, shape, dt))

        def sem(name):
            return ctx.enter_context(nc.semaphore(name))

        T8 = [128, TILES, EXPERTS]
        weight = sb("weight", T8, F32)
        ident16 = sb("e_ident16", [128, 128], F16)
        xs = [sb(f"xs_{k}", [128, SUPER, 2 * D], F16) for k in range(2)]
        xT = [sb(f"xT_{k}", [128, SUPER, 3, 128], F16) for k in range(2)]

        route(nc, router, ident, xs2_dram, weight, ident16, xs, xT)

        stage1 = [sb(f"stage1_{k}", [128, 3, FF], F32) for k in range(2)]
        stage2 = [sb(f"stage2_{k}", [128, MF, D], F32) for k in range(2)]
        w1s = [sb("w1_hi", [128, EXPERTS, 3, FF], F16), sb("w1_lo", [128, EXPERTS, 2, FF], F16)]
        w2s = [sb("w2_hi", [128, EXPERTS, MF, D], F16), sb("w2_lo", [128, EXPERTS, MF, D], F16)]
        b1s = sb("b1s", [128, EXPERTS, MF], F32)
        b2f = sb("b2f", [64, EXPERTS * D], F32)
        b2s = sb("b2s", [128, EXPERTS * D], F16)
        two_rows = sb("e_two_rows", [128, 128], F16)
        act_out = [sb(f"act_out{k}", [128, MF, NSUP], F32) for k in range(2)]
        g_hi = [sb(f"g_hi{k}", [128, MF, NSUP], F16) for k in range(2)]
        g_lo = [sb(f"g_lo{k}", [128, MF, NSUP], F16) for k in range(2)]
        acc = [sb(f"acc{k}", [128, SUPER, D], F32) for k in range(2)]

        up = [pb(f"up{k}", [128, 512], F32) for k in range(3)]
        down = [pb(f"down{k}", [128, 2, 512], F32) for k in range(2)]
        turned = pb("turned", [128, 512], F32)

        s = {n: sem("e_" + n) for n in ("bias_in memory split_hi split_lo prep turned_a turned_b xT_a xT_b up_done gelu_done "
                                        "hi_done lo_done down_done acc_done").split()}
        s_stage = [sem(f"e_stage{k}") for k in range(2)]
        s_xs = [sem(f"e_xs{k}") for k in range(2)]
        s_h2 = [sem(f"e_h2{k}") for k in range(2)]
        s_out = [sem(f"e_out{k}") for k in range(2)]
        half = MF // 2

        def rows_of(dram, st):
            if isinstance(st, int):
                return dram[st * NSUP:(st + 1) * NSUP, :].rearrange("(n p) c -> p n c", p=128)
            return dram[bass.ds(st * NSUP, NSUP), :].rearrange("(n p) c -> p n c", p=128)

        def place(n):
            return n // 2, (n % 2) * D

        block = ctx.enter_context(nc.Block())

        @block.sync
        def _(sp):
            sp.wait_ge(s["memory"], 1)
            sp.dma_start(b1s[:], b1).then_inc(s["bias_in"], 16)
            for row in (0, 32):
                sp.dma_start(b2f[row:row + 1, :], b2).then_inc(s["bias_in"], 16)
            for e in range(EXPERTS):
                if e >= 2:
                    sp.wait_ge(s["split_lo"], e - 1)
                    sp.wait_ge(s["split_hi"], e - 1)
                sp.dma_start(stage1[e % 2][:], w1[e]).then_inc(s_stage[e % 2], 16)
                sp.dma_start(stage2[e % 2][:], w2[e]).then_inc(s_stage[e % 2], 16)

            def body(st, k):
                need(sp, s["turned_b"], st - 1)
                sp.dma_start(xs[k][:], rows_of(xs2_dram, st)).then_inc(s_xs[k], 16)
                need(sp, s_out[k], 8 * (st - k))
                sp.dma_start(acc[k][:], rows_of(h2_dram, st)).then_inc(s_h2[k], 16)

            super_pipeline(sp, body)

        @block.gpsimd
        def _(pool):
            pool.memset(b2f[:], 0.0)
            pool.memset(b2s[:], 0.0)
            pool.memset(two_rows[:], 0.0).then_inc(s["memory"], 1)
            for n, row in enumerate((0, 32)):
                pool.wait_ge(s["memory"], n + 1)
                pool.memset(two_rows[row:row + 1, :], 1.0).then_inc(s["memory"], 1)

            def body(st, k):
                pool.wait_ge(s["acc_done"], EXPERTS * (st + 1))
                pool.dma_start(rows_of(out, st), acc[k][:]).then_inc(s_out[k], 16)

            super_pipeline(pool, body)
            pool.wait_ge(s_out[0], 16 * ((SUPERS + 1) // 2))
            pool.wait_ge(s_out[1], 16 * (SUPERS // 2))

        @block.scalar
        def _(act):
            for e in range(EXPERTS):
                act.wait_ge(s_stage[e % 2], 32 * (e // 2 + 1))
                act.mul(w1s[0][:, e], stage1[e % 2][:], WS)
                act.mul(w2s[0][:, e], stage2[e % 2][:], WS).then_inc(s["split_hi"], 1)
            act.wait_ge(s["bias_in"], 48)
            for row in (0, 32):
                ins = act.mul(b2s[row:row + 1, :], b2f[row:row + 1, :], WS)
            ins.then_inc(s["prep"], 1)

            def gelu(st, e, k):
                u = EXPERTS * st + e
                for m in range(MF):
                    if m % half == 0:
                        need(act, s["lo_done"], 2 * u - 3 + m // half)
                    act.wait_ge(s["up_done"], MF * u + m + 1)
                    act.activation(act_out[e % 2][:, m, :], up[m % 3][:, 0:NSUP], ACT.Gelu,
                                   bias=b1s[:, e, m:m + 1], scale=1.0 / WS).then_inc(s["gelu_done"], 1)

            def body(st, k):
                for e in range(EXPERTS):
                    gelu(st, e, k)

            super_pipeline(act, body)

        @block.vector
        def _(dve):
            for e in range(EXPERTS):
                dve.wait_ge(s["split_hi"], e + 1)
                dve.scalar_tensor_tensor(out=w1s[1][:, e], in0=stage1[e % 2][:, 0:2, :], scalar=WS, in1=w1s[0][:, e, 0:2, :],
                                         op0=ALU.mult, op1=ALU.subtract)
                dve.scalar_tensor_tensor(out=w2s[1][:, e], in0=stage2[e % 2][:], scalar=WS, in1=w2s[0][:, e],
                                         op0=ALU.mult, op1=ALU.subtract).then_inc(s["split_lo"], 1)
            dve.wait_ge(s["prep"], 1)
            dve.scalar_tensor_tensor(out=b2s[32:33, :], in0=b2f[32:33, :], scalar=WS, in1=b2s[32:33, :],
                                     op0=ALU.mult, op1=ALU.subtract).then_inc(s["prep"], 1)

            def turn_out(st, k, part):
                dve.wait_ge(s["turned_" + part], st + 1)
                need(dve, s["up_done"], EXPERTS * MF * (st - 1))
                n = slice(0, 2) if part == "a" else slice(2, 3)
                cols = 6 * 128 if part == "a" else 3 * 128
                dve.tensor_copy(xT[k][:, n].rearrange("p n c r -> p (n c r)"), turned[:].bitcast(F16)[:, 0:cols])\
                   .then_inc(s["xT_" + part], 1)

            def split(st, e):
                u = EXPERTS * st + e
                for j in range(2):
                    m = slice(half * j, half * j + half)
                    dve.wait_ge(s["gelu_done"], MF * u + half * (j + 1))
                    need(dve, s["down_done"], u - 1)
                    dve.tensor_copy(g_hi[e % 2][:, m, :], act_out[e % 2][:, m, :]).then_inc(s["hi_done"], 1)
                    dve.wait_ge(s["hi_done"], 2 * u + j + 1)
                    dve.tensor_tensor(g_lo[e % 2][:, m, :], act_out[e % 2][:, m, :], g_hi[e % 2][:, m, :],
                                      ALU.subtract).then_inc(s["lo_done"], 1)

            def combine(st, e, k, last_wait=True):
                u = EXPERTS * st + e
                dve.wait_ge(s["down_done"], u + 1)
                if e == 0:
                    dve.wait_ge(s_h2[k], 16 + 8 * (st - k))
                need(dve, s["acc_done"], u)
                for n in range(SUPER):
                    bank, at = place(n)
                    tile = SUPER * st + n
                    w = weight[:, tile, e:e + 1] if isinstance(tile, int) else weight[:, bass.ds(tile, 1), e]
                    ins = dve.scalar_tensor_tensor(out=acc[k][:, n, :], in0=down[e % 2][:, bank, at:at + D], scalar=w,
                                                   in1=acc[k][:, n, :], op0=ALU.mult, op1=ALU.add)
                ins.then_inc(s["acc_done"], 1)

            turn_out(0, 0, "a")
            turn_out(0, 0, "b")

            def body(st, k):
                last = isinstance(st, int) and st == SUPERS - 1
                first = isinstance(st, int) and st == 0
                for e in range(EXPERTS):
                    if e >= 1:
                        split(st, e)
                    elif first:
                        split(st, 0)
                    if e == 1 or e == 0:
                        pass
                    if e >= 1:
                        combine(st, e - 1, k)
                    if e == 4 and not last:
                        turn_out(st + 1, 1 - k, "a")
                    if e == 6 and not last:
                        turn_out(st + 1, 1 - k, "b")
                if not last:
                    split(st + 1, 0)
                combine(st, EXPERTS - 1, k)

            super_pipeline(dve, body)

        @block.tensor
        def _(pe):
            pe.wait_ge(s["memory"], 3)

            def turn(st, k, part):
                if part == "a":
                    pe.wait_ge(s_xs[k], 16 + 8 * (st - k))
                    need(pe, s["xT_b"], st)
                else:
                    pe.wait_ge(s["xT_a"], st + 1)
                for j, n in enumerate((0, 1) if part == "a" else (2,)):
                    for c in range(3):
                        at = (3 * j + c) * 128
                        ins = pe.transpose(turned[:].bitcast(F16)[:, at:at + 128], xs[k][:, n, 128 * c:128 * c + 128], ident16[:])
                ins.then_inc(s["turned_" + part], 1)

            def up_product(st, e, k):
                u = EXPERTS * st + e
                if e == 0:
                    pe.wait_ge(s["xT_b"], st + 1)
                for m in range(MF):
                    need(pe, s["gelu_done"], MF * u + m - 2)
                    for j, (c, w, h) in enumerate(PRODUCTS):
                        ins = pe.matmul(up[m % 3][:, 0:NSUP], w1s[h][:, e, w, 128 * m:128 * m + 128], xT[k][:, :, c, :],
                                        start=(j == 0), stop=(j == len(PRODUCTS) - 1))
                    ins.then_inc(s["up_done"], 1)

            def down_product(st, e):
                u = EXPERTS * st + e
                pe.wait_ge(s["lo_done"], 2 * u + 2)
                need(pe, s["acc_done"], u - 1)
                for n in range(SUPER):
                    bank, at = place(n)
                    dst = down[e % 2][:, bank, at:at + D]
                    pe.matmul(dst, two_rows[:], b2s[:, e * D:e * D + D], start=True, stop=False)
                    cols = slice(128 * n, 128 * n + 128)
                    for m in range(MF):
                        pe.matmul(dst, g_hi[e % 2][:, m, cols], w2s[0][:, e, m, :], start=False, stop=False)
                        pe.matmul(dst, g_hi[e % 2][:, m, cols], w2s[1][:, e, m, :], start=False, stop=False)
                        ins = pe.matmul(dst, g_lo[e % 2][:, m, cols], w2s[0][:, e, m, :], start=False, stop=(m == MF - 1))
                ins.then_inc(s["down_done"], 1)

            turn(0, 0, "a")
            turn(0, 0, "b")
            pe.wait_ge(s["split_lo"], EXPERTS)
            pe.wait_ge(s["prep"], 2)
            up_product(0, 0, 0)

            def body(st, k):
                last = isinstance(st, int) and st == SUPERS - 1
                for e in range(EXPERTS):
                    if e < EXPERTS - 1:
                        up_product(st, e + 1, k)
                    elif not last:
                        up_product(st + 1, 0, 1 - k)
                    if e == 3 and not last:
                        turn(st + 1, 1 - k, "a")
                    if e == 5 and not last:
                        turn(st + 1, 1 - k, "b")
                    down_product(st, e)

            super_pipeline(pe, body)


def route(nc, router, ident, xs2_dram, weight, ident16, xs, xT):
    with ExitStack() as ctx:
        def sb(name, shape, dt):
            return ctx.enter_context(nc.sbuf_tensor(name, shape, dt))

        def sem(name):
            return ctx.enter_context(nc.semaphore(name))

        T8 = [128, TILES, EXPERTS]
        T1 = [128, TILES]
        identf = sb("r_identf", [128, 128], F32)
        wr32 = sb("wr32", [128, 3, EXPERTS], F32)
        wr = [sb("wr_hi", [128, 3, EXPERTS], F16), sb("wr_lo", [128, 2, EXPERTS], F16)]
        logit = sb("logit", T8, F32)
        prob = sb("rprob", T8, F32)
        chosen = [sb(f"chosen{k}", T8, F32) for k in range(2)]
        tmp = sb("tmp", T8, F32)
        rank = sb("rank", [128, EXPERTS], F32)
        small = {n: sb("r_" + n, T1, F32) for n in ("top", "sum", "inv", "best", "p0", "p1")}
        tp = [ctx.enter_context(nc.psum_tensor(f"r_tp{k}", [128, 2, 512], F32)) for k in range(2)]
        lg = [ctx.enter_context(nc.psum_tensor(f"r_lg{k}", [128, 512], F32)) for k in range(2)]
        s = {n: sem("r_" + n) for n in "consts rank_set prep turned xT_set routed logit_set step exp_set".split()}
        s_xs = [sem(f"r_xs{k}") for k in range(2)]
        block = ctx.enter_context(nc.Block())

        @block.sync
        def _(sp):
            sp.dma_start(identf[:], ident).then_inc(s["consts"], 16)
            sp.dma_start(wr32[:], router).then_inc(s["consts"], 16)

            def body(st, k):
                need(sp, s["turned"], st - 1)
                src = xs2_dram[st * NSUP:(st + 1) * NSUP, :] if isinstance(st, int) else xs2_dram[bass.ds(st * NSUP, NSUP), :]
                sp.dma_start(xs[k][:], src.rearrange("(n p) c -> p n c", p=128)).then_inc(s_xs[k], 16)

            super_pipeline(sp, body)

        @block.gpsimd
        def _(pool):
            for e in range(EXPERTS):
                ins = pool.memset(rank[:, e:e + 1], float(EXPERTS - e))
            ins.then_inc(s["rank_set"], 1)

        @block.scalar
        def _(act):
            act.wait_ge(s["consts"], 32)
            act.copy(ident16[:], identf[:])
            act.mul(wr[0][:], wr32[:], WS).then_inc(s["prep"], 1)

            def body(st, k):
                act.wait_ge(s["routed"], st + 1)
                dst = logit[:, SUPER * st:SUPER * st + SUPER, :] if isinstance(st, int) else logit[:, bass.ds(SUPER * st, SUPER), :]
                act.mul(dst, lg[k][:, 0:SUPER * EXPERTS].rearrange("p (n e) -> p n e", e=EXPERTS), 1.0 / WS).then_inc(s["logit_set"], 1)

            super_pipeline(act, body)
            act.wait_ge(s["step"], 2)
            act.activation(prob[:], logit[:], ACT.Exp).then_inc(s["exp_set"], 1)

        @block.vector
        def _(dve):
            dve.wait_ge(s["prep"], 1)
            dve.scalar_tensor_tensor(out=wr[1][:], in0=wr32[:, 0:2, :], scalar=WS, in1=wr[0][:, 0:2, :],
                                     op0=ALU.mult, op1=ALU.subtract).then_inc(s["prep"], 1)

            def body(st, k):
                dve.wait_ge(s["turned"], st + 1)
                need(dve, s["routed"], st - 1)
                for n, cols in ((0, 6 * 128), (1, 3 * 128)):
                    ins = dve.tensor_copy(xT[k][:, 2 * n:2 * n + 2 - n].rearrange("p n c r -> p (n c r)"),
                                          tp[k][:, n, :].bitcast(F16)[:, 0:cols])
                ins.then_inc(s["xT_set"], 1)

            super_pipeline(dve, body)
            steps = [0]

            def then(ins):
                steps[0] += 1
                ins.then_inc(s["step"], 1)
                dve.wait_ge(s["step"], steps[0])

            def wide(a):
                return a[:].unsqueeze(2).to_broadcast(T8)

            dve.wait_ge(s["logit_set"], SUPERS)
            dve.wait_ge(s["rank_set"], 1)
            then(dve.tensor_reduce(small["top"][:], logit[:], AX.X, ALU.max))
            then(dve.tensor_tensor(logit[:], logit[:], wide(small["top"]), ALU.subtract))
            dve.wait_ge(s["exp_set"], 1)
            then(dve.tensor_reduce(small["sum"][:], prob[:], AX.X, ALU.add))
            then(dve.reciprocal(small["inv"][:], small["sum"][:]))
            then(dve.tensor_tensor(prob[:], prob[:], wide(small["inv"]), ALU.mult))
            for j in range(2):
                top = small[f"p{j}"]
                then(dve.tensor_reduce(top[:], prob[:], AX.X, ALU.max))
                then(dve.tensor_tensor(tmp[:], prob[:], wide(top), ALU.is_ge))
                then(dve.tensor_tensor(tmp[:], tmp[:], rank[:].unsqueeze(1).to_broadcast(T8), ALU.mult))
                then(dve.tensor_reduce(small["best"][:], tmp[:], AX.X, ALU.max))
                then(dve.tensor_tensor(chosen[j][:], tmp[:], wide(small["best"]), ALU.is_equal))
                if j == 0:
                    then(dve.scalar_tensor_tensor(out=prob[:].rearrange("p n e -> p (n e)"), in0=chosen[0][:].rearrange("p n e -> p (n e)"),
                                                  scalar=-2.0, in1=prob[:].rearrange("p n e -> p (n e)"), op0=ALU.mult, op1=ALU.add))
            then(dve.tensor_tensor(small["sum"][:], small["p0"][:], small["p1"][:], ALU.add))
            then(dve.reciprocal(small["inv"][:], small["sum"][:]))
            for j in range(2):
                then(dve.scalar_tensor_tensor(out=small[f"p{j}"][:], in0=small[f"p{j}"][:], scalar=1.0 / WS,
                                              in1=small["inv"][:], op0=ALU.mult, op1=ALU.mult))
                then(dve.tensor_tensor(chosen[j][:], chosen[j][:], wide(small[f"p{j}"]), ALU.mult))
            then(dve.tensor_tensor(weight[:], chosen[0][:], chosen[1][:], ALU.add))

        @block.tensor
        def _(pe):
            pe.wait_ge(s["prep"], 2)

            def body(st, k):
                pe.wait_ge(s_xs[k], 16 + 8 * (st - k))
                need(pe, s["xT_set"], st - 1)
                for n in range(SUPER):
                    for c in range(3):
                        at = (3 * (n % 2) + c) * 128
                        ins = pe.transpose(tp[k][:, n // 2, :].bitcast(F16)[:, at:at + 128], xs[k][:, n, 128 * c:128 * c + 128], ident16[:])
                ins.then_inc(s["turned"], 1)
                pe.wait_ge(s["xT_set"], st + 1)
                need(pe, s["logit_set"], st - 1)
                for n in range(SUPER):
                    for j, (c, w, h) in enumerate(PRODUCTS):
                        ins = pe.matmul(lg[k][:, n * EXPERTS:(n + 1) * EXPERTS], xT[k][:, n, c, :], wr[h][:, w, :],
                                        start=(j == 0), stop=(j == len(PRODUCTS) - 1))
                ins.then_inc(s["routed"], 1)

            super_pipeline(pe, body)


def lay_out(x, L0_tok_W, L0_tok_b, L0_tok_class_token, L0_tok_pos_embed, L0_attn_w_qkv, L0_attn_w_proj,
            L0_attn_b_proj, L0_ffn_router_w, L0_ffn_w1, L0_ffn_b1, L0_ffn_w2, L0_ffn_b2):
    f = np.float32
    patches = np.asarray(x).reshape(IMGS, CHANS, NPATCH, PATCH, NPATCH, PATCH).transpose(0, 1, 3, 5, 2, 4)
    patches = patches.reshape(IMGS, KIN, 128, SEQ - 1).transpose(0, 2, 1, 3)
    xt = np.zeros((IMGS, 128, KIN, SEQ), f)
    xt[..., 1:] = patches

    def two_tiles(a):
        return np.ascontiguousarray(np.stack([a[at:at + ROWS] for at in TILE_AT], axis=1))

    def stacked(w):
        return np.ascontiguousarray(np.asarray(w)[np.array(STACK)].transpose(1, 0, 2))

    bias_tab = np.concatenate([np.asarray(L0_tok_class_token), np.repeat(np.asarray(L0_tok_b)[None], SEQ - 1, 0)])
    qkv = np.asarray(L0_attn_w_qkv)
    cols = [which * D + (g * HPG + h) * DH + d for which in range(2) for g in range(GROUPS) for h in range(HPG)
            for _ in range(2) for d in range(DH)]
    r, c = np.arange(ROWS)[:, None], np.arange(KEYS)[None]
    band = np.stack([np.where(abs((c + KEYS_AT[n]) - (r + TILE_AT[n])) <= HALF_WIN, 0.0, MASKED) for n in range(2)], 1)
    return {
        "xt": xt,
        "w_embed": np.asarray(L0_tok_W).T.reshape(KIN, 128, D).transpose(1, 0, 2),
        "bias_tab": two_tiles(bias_tab),
        "pos": two_tiles(np.asarray(L0_tok_pos_embed)),
        "w_qk": stacked(qkv[:, cols]),
        "w_v": stacked(qkv[:, 2 * D:]),
        "w_p": stacked(L0_attn_w_proj),
        "b_p": np.asarray(L0_attn_b_proj)[None],
        "router": stacked(np.asarray(L0_ffn_router_w).T),
        "w1": np.stack([stacked(w) for w in np.asarray(L0_ffn_w1)]),
        "b1": np.asarray(L0_ffn_b1).reshape(EXPERTS, MF, 128).transpose(2, 0, 1),
        "w2": np.asarray(L0_ffn_w2).reshape(EXPERTS, MF, 128, D).transpose(0, 2, 1, 3),
        "b2": np.asarray(L0_ffn_b2).reshape(1, EXPERTS * D),
        "ident": np.eye(128, dtype=f),
        "band": band.astype(f),
        "low_rows": -(np.arange(128) % 32 >= DH).astype(f)[:, None],
    }


def kernel(**inputs):
    import concourse.bacc as bacc
    from concourse.bass_utils import run_bass_kernel_spmd

    nc = bacc.Bacc("TRN2", target_bir_lowering=False, num_devices=1)
    arrays, args = {}, {}
    for name, a in lay_out(**inputs).items():
        a = np.ascontiguousarray(a)
        arrays[f"in_{name}"] = a
        args[name] = nc.dram_tensor(f"in_{name}", a.shape, mybir.dt.from_np(a.dtype), kind="ExternalInput").ap()
    args["out"] = nc.dram_tensor("out_0", (PAD_TOKENS, D), F32, kind="ExternalOutput").ap()
    vit_tower(nc, **args)
    result = run_bass_kernel_spmd(nc, [arrays], core_ids=[0])
    return result.results[0]["out_0"][:TOKENS].reshape(IMGS, SEQ, D)
```

```python
from contextlib import ExitStack

import numpy as np

import concourse.bass as bass
from concourse import mybir

F32 = mybir.dt.float32
F16 = mybir.dt.float16
BF16 = mybir.dt.bfloat16
U16 = mybir.dt.uint16
U32 = mybir.dt.uint32
ALU = mybir.AluOpType
ACT = mybir.ActivationFunctionType
AX = mybir.AxisListType

IMGS, CHANS, SIDE, NPATCH = 64, 3, 224, 14
PATCH = SIDE // NPATCH
SEQ = NPATCH * NPATCH + 1
D = 192
DIN = CHANS * PATCH * PATCH
KIN = DIN // 128
HEADS, DH = 12, 16
GROUPS = 3
HPG = HEADS // GROUPS
HALF_WIN = 6
ROWS = (SEQ + 1) // 2
SPAN = 2 * ROWS
PITCH = ROWS + ROWS % 2
TILE_ROWS = (ROWS, SEQ - ROWS)
KEYS = ROWS + HALF_WIN
KEYS_AT = (0, SPAN - KEYS)
EXPERTS, FF = 8, 768
MF = FF // 128
WS = 64.0
EPS = 1e-5
MASKED = -1e30
CHOSEN = 2
TOKENS = IMGS * SEQ
NUMBER_AT = 2 * D
WEIGHT_AT = NUMBER_AT + 2
PAYLOAD = WEIGHT_AT + 2 * EXPERTS
BATCH = 512
PARTS = BATCH // 128
REGION = TOKENS + BATCH
SPARE = EXPERTS * REGION
BATCHES = (CHOSEN * TOKENS + EXPERTS * (BATCH - 1)) // BATCH
BATCHES += (2 - BATCHES) % 4
STEPS = 31
PART_AT = (0, 2, 16, STEPS)

STACK = [list(range(128)), list(range(128, 192)) + list(range(64)), list(range(64, 192))]
PRODUCTS = [(0, 0, 0), (1, 1, 0), (2, 2, 0), (0, 0, 1), (1, 1, 1)]


def need(eng, sem, value):
    if not isinstance(value, int) or value > 0:
        eng.wait_ge(sem, value)


def need_apart(eng, sem, value, met):
    eng.wait_ge(*met)
    eng.wait_ge(sem, value)


def pipeline(eng, body):
    for t in range(8):
        body(t, t % 4, t // 4)
    with eng.Fori(2, IMGS // 4) as p:
        for k in range(4):
            body(4 * p + k, k, p)
    for t in range(IMGS, IMGS + 4):
        body(t, t % 4, t // 4)


def runs(t):
    if isinstance(t, int):
        return [lag <= t < IMGS + lag for lag in range(4)] + [5 <= t < IMGS + 4]
    return [True] * 5


def vit_tower(nc, xt, w_embed, bias_tab, pos, w_qk, w_v, w_p, b_p, router, w1, b1, w2, b2,
              ident, band, low_rows, above, numbers, token_no, fill, region_at, out):
    sorted_dram = nc.dram_tensor("sorted_scratch", (SPARE + BATCH, PAYLOAD), U16).ap()
    with ExitStack() as ctx:
        def sb(name, shape, dt):
            return ctx.enter_context(nc.sbuf_tensor(name, shape, dt))

        region_end = [sb(f"region_end{k}", [128, EXPERTS], F32) for k in range(2)]
        ident16 = sb("ident16", [128, 128], F16)
        attention_part(nc, xt, w_embed, bias_tab, pos, w_qk, w_v, w_p, b_p, router, ident, band, low_rows,
                       above, token_no, region_at, region_end, ident16, sorted_dram, out)
        batch_row = sb("batch_row", [1, BATCHES], mybir.dt.int32)
        batch_expert = sb("batch_expert", [1, BATCHES], mybir.dt.int32)
        w1s = [sb("w1_hi", [128, EXPERTS, 3, FF], F16), sb("w1_lo", [128, EXPERTS, 2, FF], F16)]
        w2s = [sb("w2_hi", [128, EXPERTS, MF, D], F16), sb("w2_lo", [128, EXPERTS, MF, D], F16)]
        b1s = sb("b1s", [128, EXPERTS, MF], F32)
        b2s = sb("b2s", [128, EXPERTS, D], F16)
        two_rows = sb("e_two_rows", [128, 128], F16)
        prepare_part(nc, w1, b1, w2, b2, numbers, fill, region_at, region_end[IMGS // CHOSEN % 2], batch_row, batch_expert,
                     sorted_dram, w1s, w2s, b1s, b2s, two_rows, out)
        experts_part(nc, sorted_dram, batch_row, batch_expert, ident16, w1s, w2s, b1s, b2s, two_rows, out)


def attention_part(nc, xt, w_embed, bias_tab, pos, w_qk, w_v, w_p, b_p, router, ident, band, low_rows,
                   above, token_no, region_at, region_end, ident16, sorted_dram, out):
    with ExitStack() as ctx:
        def sb(name, shape, dt):
            return ctx.enter_context(nc.sbuf_tensor(name, shape, dt))

        def pb(name, shape, dt):
            return ctx.enter_context(nc.psum_tensor(name, shape, dt))

        def sem(name):
            return ctx.enter_context(nc.semaphore(name))

        identf = sb("identf", [128, 128], F32)
        identb = sb("identb", [128, 128], BF16)
        above32 = sb("above32", [128, 128], F32)
        above16 = sb("above16", [128, 128], F16)
        ones16 = sb("ones16", [128, 128], F16)
        rank = sb("rank", [ROWS, EXPERTS], F32)
        tokens = sb("tokens", [ROWS, IMGS, 2], F32)
        bandf = sb("bandf", [ROWS, 2, KEYS], F32)
        bandb = sb("bandb", [ROWS, 2, KEYS], BF16)
        low = sb("low", [128, 1], F32)
        we = sb("we", [128, KIN, D], F32)
        tab = sb("tab", [ROWS, 2, D], F32)
        post = sb("post", [ROWS, 2, D], F32)
        weights32, weights16 = {}, {}
        for name, cols in (("wqk", 2 * GROUPS * 128), ("wv", D), ("wp", D), ("wr", EXPERTS)):
            weights32[name] = sb(name + "32", [128, 3, cols], F32)
            weights16[name] = [sb(name + "_hi", [128, 3, cols], F16), sb(name + "_lo", [128, 2, cols], F16)]
        wqk, wv, wp, wr = weights16.values()
        bp32 = sb("bp32", [64, D], F32)
        bp = sb("bp", [128, D], F16)
        two_rows = sb("two_rows", [128, 128], F16)
        carrier = sb("carrier", [32, 2], F32)
        half_pow = sb("half_pow", [128, 2], F32)
        eps = sb("eps", [128, 2], F32)

        patches = [sb(f"patches{k}", [128, KIN, SPAN], F32) for k in range(2)]
        h1 = [sb(f"h1_{k}", [ROWS, 2, D], F32) for k in range(4)]
        st1 = sb("st1", [ROWS, 2, 6], F32)
        mv1 = sb("mv1", [ROWS, 2, 2], F32)
        rs1 = sb("rs1", [ROWS, 2], F32)
        xn1 = sb("xn1", [ROWS, 2, D], F32)
        xs1 = sb("xs1", [ROWS, 2, 2 * D], F16)
        xT1 = sb("xT1", [128, 3, SPAN], F16)
        qk_hi = sb("qk_hi", [128, GROUPS, 2, SPAN], F16)
        q_lo = sb("q_lo", [128, GROUPS, SPAN], F16)
        k_st = sb("k_st", [128, GROUPS, SPAN], F16)
        k_diag = sb("k_diag", [128, GROUPS, HPG, SPAN], F16)

        v_hi = sb("v_hi", [KEYS, 2, HEADS, DH + 1], F16)
        v_lo = sb("v_lo", [KEYS, 2, HEADS, DH + 1], F16)
        mx = [sb(f"mx{k}", [ROWS, GROUPS, HPG], F32) for k in range(2)]
        prob = [sb(f"prob{k}", [ROWS, GROUPS, HPG, KEYS], F32) for k in range(2)]
        pT_hi = [sb(f"pT_hi{k}", [KEYS, GROUPS, HPG * ROWS], F16) for k in range(2)]
        pT_lo = [sb(f"pT_lo{k}", [KEYS, GROUPS, HPG * ROWS], F16) for k in range(2)]
        rden = sb("rden", [ROWS, 2, HEADS], F32)
        on = sb("on", [ROWS, 2, D], F32)
        os_ = sb("os", [ROWS, 2, 2 * D], F16)

        oT = sb("oT", [128, 2, 3, ROWS], F16)
        h2 = [sb(f"h2_{k}", [ROWS, 2, D], F32) for k in range(2)]
        st2 = sb("st2", [ROWS, 2, 6], F32)
        mv2 = sb("mv2", [ROWS, 2, 2], F32)
        rs2 = sb("rs2", [ROWS, 2], F32)
        xn2 = sb("xn2", [ROWS, 2, D], F32)
        xT2 = sb("xT2", [128, 2, 3, ROWS], F16)
        payload = [sb(f"payload{k}", [ROWS, 4, PAYLOAD], U16) for k in range(2)]

        T8 = [ROWS, 4, EXPERTS]
        logit = sb("logit", T8, F32)
        rprob = sb("rprob", T8, F32)
        chosen = [sb(f"chosen{k}", T8, F32) for k in range(CHOSEN)]
        scaled = [sb(f"scaled{k}", T8, F32) for k in range(CHOSEN)]
        tmp = sb("tmp", T8, F32)
        marks = sb("marks", T8, F16)
        small = {n: sb("r_" + n, [ROWS, 4], F32) for n in ("top", "sum", "inv", "best", "p0", "p1")}
        place_f = sb("place_f", [ROWS, 4, CHOSEN], F32)
        place = [sb(f"place{k}", [ROWS, 4, CHOSEN], U32) for k in range(2)]

        big = [pb(f"big{k}", [128, 3, 512], F32) for k in range(2)]
        one = [pb(f"one{k}", [128, 512], F32) for k in range(2)]

        names = ("load_c zero_mem weights embedded h1_set stats1 aggr1 rstd1 normed1 hi1 lo1 turned1 xT_set qk_done "
                 "qk_hi_set q_lo_set k_st_set v_done v_hi_set v_lo_set norm_done o_hi_set k_diag_a k_diag_b "
                 "o_lo_set o_turned oT_set proj_done h2_set stats2 aggr2 rstd2 normed2 hi2 lo2 den_set "
                 "pv_done var1 var2 setup1 setup2 turned2 xT2_set routed logit_set step exp_set marks_set counted carried").split()
        s = {n: sem(n) for n in names}
        s_max, s_score, s_sub, s_exp, s_pT, s_phi, s_plo = (
            [sem(f"{n}{k}") for k in range(2)]
            for n in ("max_set", "scored", "shifted", "exp_set", "prob_turned", "p_hi_set", "p_lo_set"))
        s_patch = [sem(f"patches_in{k}") for k in range(2)]
        s_h2out = [sem(f"h2_out{k}") for k in range(2)]
        s_sent = [sem(f"sent{k}") for k in range(2)]
        SENT = 16 * 4 * CHOSEN
        LOADS = 16 * 14

        block = ctx.enter_context(nc.Block())

        @block.sync
        def _(sp):
            for dst, src in ((we[:], w_embed), (tab[:], bias_tab), (post[:], pos), (identf[:], ident), (bandf[:], band),
                             (low[:], low_rows), (weights32["wqk"][:], w_qk), (weights32["wv"][:], w_v),
                             (weights32["wp"][:], w_p), (weights32["wr"][:], router), (above32[:], above), (tokens[:], token_no)):
                sp.dma_start(dst, src).then_inc(s["load_c"], 16)
            sp.dma_start(region_end[0][:], region_at).then_inc(s["load_c"], 16)
            sp.wait_ge(s["zero_mem"], 1)
            for n, row in enumerate((0, 32)):
                sp.dma_start(bp32[row:row + 1, :], b_p).then_inc(s["setup1"], 16)

            def body(t, k, p):
                embed, project, attention, back, route = runs(t)
                if embed:
                    need(sp, s["embedded"], t - 1)
                    src = xt[t:t + 1] if isinstance(t, int) else xt[bass.ds(t, 1)]
                    sp.dma_start(patches[k % 2][:], src.rearrange("a p k n -> p (a k) n")).then_inc(s_patch[k % 2], 16)
                if project:
                    f = t - 1
                    sp.wait_ge(s["k_st_set"], f + 1)
                    need(sp, s_score[1], f)
                    for h in range(HPG):
                        q = slice(32 * h, 32 * h + 32)
                        sp.dma_start(k_diag[q, :, h, :], k_st[q, :, :]).then_inc(s["k_diag_a"], 16)

            pipeline(sp, body)

        @block.gpsimd
        def _(pool):
            pool.memset(bp32[:], 0.0)
            pool.memset(bp[:], 0.0)
            pool.memset(two_rows[:], 0.0)
            pool.memset(ones16[:], 1.0)
            pool.memset(half_pow[:], -0.5)
            pool.memset(eps[:], EPS)
            pool.memset(carrier[:], 0.0)
            pool.memset(v_hi[:], WS)
            pool.memset(v_lo[:], 0.0)
            for e in range(EXPERTS):
                pool.memset(rank[:, e:e + 1], float(EXPERTS - e))
            pool.memset(k_diag[:], 0.0).then_inc(s["zero_mem"], 1)
            pool.wait_ge(s["zero_mem"], 1)
            for n, row in enumerate((0, 32)):
                pool.memset(two_rows[row:row + 1, :], 1.0).then_inc(s["zero_mem"], 1)
                pool.wait_ge(s["zero_mem"], n + 2)

            def rsqrt(n_th, mv, rs, aggr, var, rstd, read):
                pool.wait_ge(s[aggr], n_th)
                pool.tensor_tensor(mv[:, :, 1], mv[:, :, 1], eps[0:ROWS, :], ALU.add).then_inc(s[var], 1)
                pool.wait_ge(s[var], n_th)
                need(pool, s[read], n_th - 1)
                pool.tensor_tensor(rs[:], mv[:, :, 1], half_pow[0:ROWS, :], ALU.pow).then_inc(s[rstd], 1)

            def body(t, k, p):
                embed, project, attention, back, route = runs(t)
                f, a, b = t, t - 2, t - 3
                pk, slot = (k - 3) % 4 // 2, 2 * ((k - 3) % 2)
                if back:
                    rsqrt(b + 1, mv2, rs2, "aggr2", "var2", "rstd2", "normed2")
                if embed:
                    rsqrt(f + 1, mv1, rs1, "aggr1", "var1", "rstd1", "normed1")
                if back:
                    pool.wait_ge(s["hi2"], b + 1)
                    dst = payload[pk][:, slot:slot + 2, :].bitcast(F16)
                    pool.tensor_tensor(dst[:, :, D:2 * D], xn2[:], dst[:, :, 0:D], ALU.subtract).then_inc(s["lo2"], 1)
                if embed:
                    pool.wait_ge(s["hi1"], f + 1)
                    need(pool, s["turned1"], f)
                    pool.tensor_tensor(xs1[:, :, D:], xn1[:], xs1[:, :, 0:D], ALU.subtract).then_inc(s["lo1"], 1)
                if attention:
                    pool.wait_ge(s["o_hi_set"], a + 1)
                    pool.tensor_tensor(os_[:, :, D:], on[:], os_[:, :, 0:D], ALU.subtract).then_inc(s["o_lo_set"], 1)
                if route and k % 2:
                    grp, gk = 2 * p + (k - 5) // 2, (k - 5) // 2 % 2
                    pool.wait_ge(s["step"], STEPS * (grp + 1))
                    need(pool, s["carried"], grp)
                    pool.tensor_tensor(carrier[:, 1:2], carrier[:, 0:1], carrier[:, 0:1], ALU.mult).then_inc(s["carried"], 1)
                    for n in range(4):
                        rows = TILE_ROWS[n % 2]
                        for j in range(CHOSEN):
                            pool.indirect_dma_start(out=sorted_dram, out_offset=bass.IndirectOffsetOnAxis(ap=place[gk][0:rows, n, j:j + 1], axis=0),
                                                    in_=payload[gk][0:rows, n, :], in_offset=None).then_inc(s_sent[gk], 16)

            pipeline(pool, body)
            for k in range(2):
                pool.wait_ge(s_sent[k], SENT * IMGS // 4)

        @block.scalar
        def _(act):
            act.wait_ge(s["load_c"], 16 * 13)
            act.copy(ident16[:], identf[:])
            act.copy(identb[:], identf[:])
            act.copy(above16[:], above32[:])
            act.copy(bandb[:], bandf[:]).then_inc(s["setup2"], 1)
            for name, w in weights32.items():
                act.mul(weights16[name][0][:], w[:], WS).then_inc(s["weights"], 1)
            act.wait_ge(s["setup1"], 32)
            for row in (0, 32):
                act.mul(bp[row:row + 1, :], bp32[row:row + 1, :], WS).then_inc(s["weights"], 1)

            def pieces(bank):
                return bank[:].bitcast(F16)[:, 0:6 * PITCH].rearrange("p (n c r) -> p n c r", n=2, c=3)[:, :, :, 0:ROWS]

            def body(t, k, p):
                embed, project, attention, back, route = runs(t)
                f, g, a, b = t, t - 1, t - 2, t - 3
                pk, slot = (k - 3) % 4 // 2, 2 * ((k - 3) % 2)
                if attention:
                    act.wait_ge(s_sub[0], a + 1)
                    act.activation(prob[0][:], prob[0][:], ACT.Exp, scale=DH ** -0.5 / (WS * WS)).then_inc(s_exp[0], 1)
                    act.wait_ge(s["v_done"], a + 1)
                    need(act, s["pv_done"], a)
                    act.copy(v_hi[:, :, :, 0:DH], one[0][0:KEYS, 0:2 * D].rearrange("p (n h d) -> p n h d", n=2, h=HEADS))\
                        .then_inc(s["v_hi_set"], 1)
                if back:
                    act.wait_ge(s["o_turned"], b + 1)
                    need(act, s["proj_done"], b)
                    act.copy(oT[:].rearrange("p n c r -> p (n c) r"), pieces(one[1]).rearrange("p n c r -> p (n c) r")).then_inc(s["oT_set"], 1)
                if project:
                    act.wait_ge(s["turned1"], g + 1)
                    need(act, s["v_done"], g)
                    need(act, s["qk_done"], g)
                    act.copy(xT1[:].rearrange("p c (n r) -> p n c r", n=2), pieces(one[0])).then_inc(s["xT_set"], 1)
                if attention:
                    act.wait_ge(s_sub[1], a + 1)
                    act.activation(prob[1][:], prob[1][:], ACT.Exp, scale=DH ** -0.5 / (WS * WS)).then_inc(s_exp[1], 1)
                if route and k % 2:
                    grp = 2 * p + (k - 5) // 2
                    act.wait_ge(s["step"], STEPS * grp + 2)
                    act.activation(rprob[:], logit[:], ACT.Exp).then_inc(s["exp_set"], 1)
                if attention:
                    for n in range(2):
                        act.wait_ge(s_pT[n], a + 1)
                        need(act, s["pv_done"], a)
                        act.copy(pT_hi[n][:], big[n][0:KEYS, :, 0:HPG * ROWS]).then_inc(s_phi[n], 1)
                if back:
                    act.wait_ge(s["normed2"], b + 1)
                    need(act, s_sent[pk], SENT * (p + ((k - 3) // 4)))
                    act.copy(payload[pk][:, slot:slot + 2, 0:D].bitcast(F16), xn2[:]).then_inc(s["hi2"], 1)
                if embed:
                    act.wait_ge(s["normed1"], f + 1)
                    need(act, s["turned1"], f)
                    act.copy(xs1[:, :, 0:D], xn1[:]).then_inc(s["hi1"], 1)
                if project:
                    act.wait_ge(s["qk_done"], g + 1)
                    need(act, s_score[1], g)
                    act.copy(qk_hi[:].rearrange("p g w n -> p g (w n)"), big[0][:, :, 0:2 * SPAN]).then_inc(s["qk_hi_set"], 1)
                if back:
                    act.wait_ge(s["h2_set"], b + 1)
                    for n in range(2):
                        at, rows = b * SEQ + ROWS * n, TILE_ROWS[n]
                        d = out[at:at + rows, :] if isinstance(at, int) else out[bass.ds(at, rows), :]
                        act.dma_start(d, h2[k % 2][0:rows, n, :]).then_inc(s_h2out[k % 2], 16)
                    act.wait_ge(s["turned2"], b + 1)
                    need(act, s["routed"], b)
                    act.copy(xT2[:].rearrange("p n c r -> p (n c) r"), pieces(one[0]).rearrange("p n c r -> p (n c) r")).then_inc(s["xT2_set"], 1)
                if attention:
                    act.wait_ge(s["norm_done"], a + 1)
                    need(act, s["o_turned"], a)
                    act.copy(os_[:, :, 0:D], on[:]).then_inc(s["o_hi_set"], 1)
                if back:
                    act.wait_ge(s["routed"], b + 1)
                    if k % 2:
                        need(act, s["exp_set"], 2 * p + (k - 3) // 2)
                    act.mul(logit[:, slot:slot + 2, :], one[1][0:ROWS, 0:2 * EXPERTS].rearrange("p (n e) -> p n e", n=2), 1.0 / WS)\
                       .then_inc(s["logit_set"], 1)

            pipeline(act, body)
            for k in range(2):
                act.wait_ge(s_h2out[k], 16 * IMGS)

        @block.vector
        def _(dve):
            dve.wait_ge(s["load_c"], 16 * 13)
            dve.tensor_tensor(tab[:], tab[:], post[:], ALU.add)
            for n, name in enumerate(weights32):
                dve.wait_ge(s["weights"], n + 1)
                hi, lo = weights16[name]
                dve.scalar_tensor_tensor(out=lo[:], in0=weights32[name][:, 0:2, :], scalar=WS, in1=hi[:, 0:2, :],
                                         op0=ALU.mult, op1=ALU.subtract)
            dve.wait_ge(s["weights"], 6)
            dve.scalar_tensor_tensor(out=bp[32:33, :], in0=bp32[32:33, :], scalar=WS, in1=bp[32:33, :],
                                     op0=ALU.mult, op1=ALU.subtract).then_inc(s["setup2"], 1)

            def normalise(mv, rs, xn, h):
                for n in range(2):
                    ins = dve.tensor_scalar(xn[:, n, :], h[:, n, :], mv[:, n, 0:1], rs[:, n:n + 1], ALU.subtract, ALU.mult)
                return ins

            def statistics(h, st, mv, stats, aggr, n_th):
                for n in range(2):
                    ins = dve.bn_stats(st[:, n, :], h[:, n, :])
                ins.then_inc(stats, 1)
                need_apart(dve, stats, n_th, (s["load_c"], 16))
                for n in range(2):
                    ins = dve.bn_aggr(mv[:, n, :], st[:, n, :])
                ins.then_inc(aggr, 1)

            def weights_of(n, a):
                scores = big[n][0:ROWS, :, 0:HPG * KEYS].rearrange("p g (h c) -> p g h c", h=HPG)
                dve.wait_ge(s_score[n], a + 1)
                dve.tensor_reduce(mx[n][:], scores, AX.X, ALU.max).then_inc(s_max[n], 1)
                dve.wait_ge(s_max[n], a + 1)
                need(dve, s_pT[n], a)
                dve.tensor_tensor(prob[n][:], scores, mx[n][:].unsqueeze(3).to_broadcast([ROWS, GROUPS, HPG, KEYS]),
                                  ALU.subtract).then_inc(s_sub[n], 1)

            def wide(x):
                return x[:].unsqueeze(2).to_broadcast(T8)

            def route_steps(grp, gk, part):
                count = [PART_AT[part]]

                def then(ins):
                    count[0] += 1
                    ins.then_inc(s["step"], 1)
                    dve.wait_ge(s["step"], STEPS * grp + count[0])

                if part == 0:
                    dve.wait_ge(s["logit_set"], 2 * grp + 2)
                    then(dve.tensor_reduce(small["top"][:], logit[:], AX.X, ALU.max))
                    then(dve.tensor_tensor(logit[:], logit[:], wide(small["top"]), ALU.subtract))
                if part == 1:
                    dve.wait_ge(s["exp_set"], grp + 1)
                    then(dve.tensor_reduce(small["sum"][:], rprob[:], AX.X, ALU.add))
                    then(dve.reciprocal(small["inv"][:], small["sum"][:]))
                    then(dve.tensor_tensor(rprob[:], rprob[:], wide(small["inv"]), ALU.mult))
                    for j in range(CHOSEN):
                        top = small[f"p{j}"]
                        then(dve.tensor_reduce(top[:], rprob[:], AX.X, ALU.max))
                        then(dve.tensor_tensor(tmp[:], rprob[:], wide(top), ALU.is_ge))
                        then(dve.tensor_tensor(tmp[:], tmp[:], rank[:].unsqueeze(1).to_broadcast(T8), ALU.mult))
                        then(dve.tensor_reduce(small["best"][:], tmp[:], AX.X, ALU.max))
                        then(dve.tensor_tensor(chosen[j][:], tmp[:], wide(small["best"]), ALU.is_equal))
                        if j == 0:
                            then(dve.scalar_tensor_tensor(out=rprob[:], in0=chosen[0][:], scalar=-2.0, in1=rprob[:], op0=ALU.mult, op1=ALU.add))
                    dve.tensor_tensor(marks[:], chosen[0][:], chosen[1][:], ALU.add).then_inc(s["marks_set"], 1)
                if part == 2:
                    then(dve.tensor_tensor(small["sum"][:], small["p0"][:], small["p1"][:], ALU.add))
                    then(dve.reciprocal(small["inv"][:], small["sum"][:]))
                    for j in range(CHOSEN):
                        then(dve.scalar_tensor_tensor(out=small[f"p{j}"][:], in0=small[f"p{j}"][:], scalar=1.0 / WS,
                                                      in1=small["inv"][:], op0=ALU.mult, op1=ALU.mult))
                        then(dve.tensor_tensor(scaled[j][:], chosen[j][:], wide(small[f"p{j}"]), ALU.mult))
                    then(dve.tensor_tensor(payload[gk][:, :, WEIGHT_AT:PAYLOAD].bitcast(F32), scaled[0][:], scaled[1][:], ALU.add))
                    img = tokens[:, 2 * grp:2 * grp + 2, :] if isinstance(grp, int) else tokens[:, bass.ds(2 * grp, 2), :]
                    then(dve.tensor_scalar(payload[gk][:, :, NUMBER_AT:WEIGHT_AT].bitcast(U32).rearrange("p (i n) c -> p i (n c)", i=2), img, 0.0, None, ALU.add))
                    dve.wait_ge(s["counted"], grp + 1)
                    counts = one[1][0:ROWS, 0:5 * EXPERTS].rearrange("p (n e) -> p n e", e=EXPERTS)
                    old, new = region_end[gk], region_end[1 - gk]
                    then(dve.tensor_tensor(tmp[:], counts[:, 0:4, :], old[0:ROWS, :].unsqueeze(1).to_broadcast(T8), ALU.add))
                    then(dve.tensor_tensor(new[0:ROWS, :], counts[:, 4, :], old[0:ROWS, :], ALU.add))
                    for j in range(CHOSEN):
                        then(dve.tensor_tensor(chosen[j][:], chosen[j][:], tmp[:], ALU.mult))
                        then(dve.tensor_reduce(place_f[:, :, j], chosen[j][:], AX.X, ALU.add))
                    then(dve.tensor_scalar(place[gk][:], place_f[:], 0.0, None, ALU.add))
                assert count[0] == PART_AT[part + 1], count[0]

            def body(t, k, p):
                embed, project, attention, back, route = runs(t)
                f, g, a, b = t, t - 1, t - 2, t - 3
                if attention:
                    weights_of(0, a)
                    dve.wait_ge(s["v_hi_set"], a + 1)
                    need(dve, s["pv_done"], a)
                    dve.tensor_tensor(v_lo[:, :, :, 0:DH], one[0][0:KEYS, 0:2 * D].rearrange("p (n h d) -> p n h d", n=2, h=HEADS),
                                      v_hi[:, :, :, 0:DH], ALU.subtract).then_inc(s["v_lo_set"], 1)
                    weights_of(1, a)
                if route and k % 2:
                    route_steps(2 * p + (k - 5) // 2, (k - 5) // 2 % 2, 0)
                if back:
                    dve.wait_ge(s["proj_done"], b + 1)
                    need(dve, s_h2out[k % 2], 16 * (b - (k - 3) % 2))
                    dve.scalar_tensor_tensor(out=h2[k % 2][:].rearrange("p n c -> p (n c)"), in0=one[1][0:ROWS, 0:2 * D], scalar=1.0 / WS,
                                             in1=h1[(k - 3) % 4][:].rearrange("p n c -> p (n c)"), op0=ALU.mult, op1=ALU.add).then_inc(s["h2_set"], 1)
                    dve.wait_ge(s["h2_set"], b + 1)
                    need(dve, s["rstd2"], b)
                    statistics(h2[k % 2], st2, mv2, s["stats2"], s["aggr2"], b + 1)
                if embed:
                    dve.wait_ge(s["embedded"], f + 1)
                    dve.tensor_tensor(h1[k][:], one[0][0:ROWS, 0:2 * D].rearrange("p (n c) -> p n c", n=2), tab[:],
                                      ALU.add).then_inc(s["h1_set"], 1)
                    dve.wait_ge(s["h1_set"], f + 1)
                    need(dve, s["rstd1"], f)
                    statistics(h1[k], st1, mv1, s["stats1"], s["aggr1"], f + 1)
                if attention:
                    for n in range(2):
                        dve.wait_ge(s_phi[n], a + 1)
                        need(dve, s["pv_done"], a)
                        dve.tensor_tensor(pT_lo[n][:], big[n][0:KEYS, :, 0:HPG * ROWS], pT_hi[n][:], ALU.subtract)\
                            .then_inc(s_plo[n], 1)
                if back:
                    dve.wait_ge(s["rstd2"], b + 1)
                    need(dve, s["lo2"], b)
                    normalise(mv2, rs2, xn2, h2[k % 2]).then_inc(s["normed2"], 1)
                if embed:
                    dve.wait_ge(s["rstd1"], f + 1)
                    need(dve, s["lo1"], f)
                    normalise(mv1, rs1, xn1, h1[k]).then_inc(s["normed1"], 1)
                if project:
                    dve.wait_ge(s["qk_hi_set"], g + 1)
                    need(dve, s_score[1], g)
                    need(dve, s["k_diag_a"], 16 * HPG * g)
                    dve.scalar_tensor_tensor(out=k_st[:], in0=qk_hi[:, :, 1, :], scalar=low[:, 0:1],
                                             in1=big[0][:, :, SPAN:2 * SPAN], op0=ALU.mult, op1=ALU.add).then_inc(s["k_st_set"], 1)
                    dve.tensor_tensor(q_lo[:], big[0][:, :, 0:SPAN], qk_hi[:, :, 0, :], ALU.subtract).then_inc(s["q_lo_set"], 1)
                if attention:
                    dve.wait_ge(s["pv_done"], a + 1)
                    o = one[1][0:ROWS, 0:2 * HEADS * (DH + 1)].rearrange("p (n h d) -> p n h d", n=2, h=HEADS)
                    dve.reciprocal(rden[:], o[:, :, :, DH]).then_inc(s["den_set"], 1)
                    dve.wait_ge(s["den_set"], a + 1)
                    need(dve, s["o_lo_set"], a)
                    dve.tensor_tensor(on[:].rearrange("p n (h d) -> p n h d", h=HEADS), o[:, :, :, 0:DH],
                                      rden[:].unsqueeze(3).to_broadcast([ROWS, 2, HEADS, DH]), ALU.mult).then_inc(s["norm_done"], 1)
                if route and k % 2:
                    for part in (1, 2):
                        route_steps(2 * p + (k - 5) // 2, (k - 5) // 2 % 2, part)

            pipeline(dve, body)

        @block.tensor
        def _(pe):
            pe.wait_ge(s["zero_mem"], 3)
            pe.wait_ge(s["setup2"], 2)

            def turn(src, dst):
                for n in range(2):
                    for c in range(3):
                        at = (3 * n + c) * PITCH
                        ins = pe.transpose(dst[:, at:at + ROWS], src[:, n, 128 * c:128 * c + 128], ident16[0:ROWS, 0:ROWS])
                return ins

            def body(t, k, p):
                embed, project, attention, back, route = runs(t)
                f, g, a, b = t, t - 1, t - 2, t - 3
                pk, slot = (k - 3) % 4 // 2, 2 * ((k - 3) % 2)
                if attention:
                    pe.wait_ge(s["k_diag_a"], 16 * HPG * (a + 1))
                    pe.wait_ge(s["q_lo_set"], a + 1)
                    for n in range(2):
                        need(pe, s_plo[n], a)
                        for j in range(GROUPS):
                            dst = big[n][0:ROWS, j, 0:HPG * KEYS]
                            keys = k_diag[:, j, :, KEYS_AT[n]:KEYS_AT[n] + KEYS]
                            rows = slice(n * ROWS, n * ROWS + ROWS)
                            pe.matmul(dst, identb[0:ROWS, 0:ROWS],
                                      bandb[:, n, :].unsqueeze(1).to_broadcast([ROWS, HPG, KEYS]), start=True, stop=False)
                            pe.matmul(dst, qk_hi[:, j, 0, rows], keys, start=False, stop=False)
                            ins = pe.matmul(dst, q_lo[:, j, rows], keys, start=False, stop=True)
                        ins.then_inc(s_score[n], 1)
                    need(pe, s["xT2_set"], b)
                    for n in range(2):
                        for j, (c, w, half) in enumerate(PRODUCTS):
                            ins = pe.matmul(one[0][0:KEYS, n * D:n * D + D], xT1[:, c, KEYS_AT[n]:KEYS_AT[n] + KEYS],
                                            wv[half][:, w, :], start=(j == 0), stop=(j == len(PRODUCTS) - 1))
                    ins.then_inc(s["v_done"], 1)
                if back:
                    pe.wait_ge(s["o_lo_set"], b + 1)
                    need(pe, s["logit_set"], b)
                    if k % 2 == 0 and not (isinstance(t, int) and t < 6):
                        pe.wait_ge(s["step"], STEPS * (2 * p + (k - 6) // 2 + 1))
                    turn(os_, one[1][:].bitcast(F16)).then_inc(s["o_turned"], 1)
                if project:
                    pe.wait_ge(s["lo1"], g + 1)
                    need(pe, s["v_lo_set"], g)
                    turn(xs1, one[0][:].bitcast(F16)).then_inc(s["turned1"], 1)
                if back:
                    pe.wait_ge(s["oT_set"], b + 1)
                    for n in range(2):
                        dst = one[1][0:ROWS, n * D:n * D + D]
                        pe.matmul(dst, two_rows[:, 0:ROWS], bp[:], start=True, stop=False)
                        for j, (c, w, half) in enumerate(PRODUCTS):
                            ins = pe.matmul(dst, oT[:, n, c, :], wp[half][:, w, :], start=False, stop=(j == len(PRODUCTS) - 1))
                    ins.then_inc(s["proj_done"], 1)
                if embed:
                    pe.wait_ge(s_patch[k % 2], 16 + 8 * (f - k % 2))
                    need(pe, s["xT_set"], g + 1)
                    for n in range(2):
                        for c in range(KIN):
                            ins = pe.matmul(one[0][0:ROWS, n * D:n * D + D], patches[k % 2][:, c, n * ROWS:n * ROWS + ROWS],
                                            we[:, c, :], start=(c == 0), stop=(c == KIN - 1))
                    ins.then_inc(s["embedded"], 1)
                if attention:
                    for n in range(2):
                        pe.wait_ge(s_exp[n], a + 1)
                        for j in range(GROUPS):
                            for h in range(HPG):
                                ins = pe.transpose(big[n][0:KEYS, j, h * ROWS:h * ROWS + ROWS], prob[n][:, j, h, :],
                                                   identf[0:ROWS, 0:ROWS])
                        ins.then_inc(s_pT[n], 1)
                if project:
                    pe.wait_ge(s["xT_set"], g + 1)
                    need(pe, s_plo[0], a + 1)
                    for j in range(GROUPS):
                        for which in range(2):
                            for i, (c, w, half) in enumerate(PRODUCTS):
                                col = (which * GROUPS + j) * 128
                                ins = pe.matmul(big[0][:, j, which * SPAN:(which + 1) * SPAN], wqk[half][:, w, col:col + 128],
                                                xT1[:, c, :], start=(i == 0), stop=(i == len(PRODUCTS) - 1))
                    ins.then_inc(s["qk_done"], 1)
                if back:
                    pe.wait_ge(s["lo2"], b + 1)
                    if embed:
                        pe.wait_ge(s["h1_set"], f + 1)
                    turn(payload[pk][:, slot:slot + 2, :].bitcast(F16), one[0][:].bitcast(F16)).then_inc(s["turned2"], 1)
                if attention:
                    need(pe, s["h2_set"], b + 1)
                    need(pe, s["v_lo_set"], a + 1)
                    for n in range(2):
                        pe.wait_ge(s_plo[n], a + 1)
                        for h in range(HEADS):
                            j, cols = h // HPG, slice((h % HPG) * ROWS, (h % HPG + 1) * ROWS)
                            at = (n * HEADS + h) * (DH + 1)
                            dst = one[1][0:ROWS, at:at + DH + 1]
                            pe.matmul(dst, pT_hi[n][:, j, cols], v_hi[:, n, h, :], start=True, stop=False)
                            pe.matmul(dst, pT_hi[n][:, j, cols], v_lo[:, n, h, :], start=False, stop=False)
                            ins = pe.matmul(dst, pT_lo[n][:, j, cols], v_hi[:, n, h, :], start=False, stop=True)
                    ins.then_inc(s["pv_done"], 1)
                if back:
                    pe.wait_ge(s["xT2_set"], b + 1)
                    need(pe, s["norm_done"], a + 1 if attention else IMGS)
                    for n in range(2):
                        for j, (c, w, half) in enumerate(PRODUCTS):
                            ins = pe.matmul(one[1][0:ROWS, n * EXPERTS:(n + 1) * EXPERTS], xT2[:, n, c, :], wr[half][:, w, :],
                                            start=(j == 0), stop=(j == len(PRODUCTS) - 1))
                    ins.then_inc(s["routed"], 1)
                if route and k % 2:
                    grp = 2 * p + (k - 5) // 2
                    pe.wait_ge(s["marks_set"], grp + 1)
                    if back:
                        pe.wait_ge(s["logit_set"], b + 1)
                    for n in range(5):
                        dst = one[1][0:ROWS, n * EXPERTS:(n + 1) * EXPERTS]
                        for i in range(min(n + 1, 4)):
                            rows = TILE_ROWS[i % 2]
                            ins = pe.matmul(dst, (above16 if i == n else ones16)[0:rows, 0:ROWS], marks[0:rows, i, :],
                                            start=(i == 0), stop=(i == min(n, 3)))
                    ins.then_inc(s["counted"], 1)

            pipeline(pe, body)




def prepare_part(nc, w1, b1, w2, b2, numbers, fill, region_at, region_end, batch_row, batch_expert,
                 sorted_dram, w1s, w2s, b1s, b2s, two_rows, out):
    with ExitStack() as ctx:
        def sb(name, shape, dt):
            return ctx.enter_context(nc.sbuf_tensor(name, shape, dt))

        def sem(name):
            return ctx.enter_context(nc.semaphore(name))

        I32 = mybir.dt.int32
        MAP = [1, BATCHES, EXPERTS]
        stage1 = [sb(f"stage1_{k}", [128, 3, FF], F32) for k in range(2)]
        stage2 = [sb(f"stage2_{k}", [128, MF, D], F32) for k in range(2)]
        b2f = sb("b2f", [64, EXPERTS, D], F32)
        zero_rows = sb("zero_rows", [128, PARTS, D], F32)
        fill_rows = sb("fill_rows", [128, PARTS, PAYLOAD], U16)
        number = sb("number", [1, BATCHES], F32)
        base = sb("base", [1, EXPERTS], F32)
        count = sb("count", [1, EXPERTS], F32)
        count_i = sb("count_i", [1, EXPERTS], I32)
        end_i = sb("end_i", [1, EXPERTS], I32)
        ends = sb("ends", [1, EXPERTS + 1], F32)
        first = sb("first", [1, EXPERTS], F32)
        begun, passed = sb("begun", MAP, F32), sb("passed", MAP, F32)
        sums = [sb(f"sums{k}", [1, BATCHES], F32) for k in range(3)]
        s = {n: sem("p_" + n) for n in "memory consts bias_in split_hi split_lo bias_hi end_set step filled".split()}
        s_stage = [sem(f"p_stage{k}") for k in range(2)]
        block = ctx.enter_context(nc.Block())

        @block.sync
        def _(sp):
            for dst, src in ((number[:], numbers), (base[:], region_at[0:1, :]), (fill_rows[:], fill)):
                sp.dma_start(dst, src).then_inc(s["consts"], 16)
            sp.wait_ge(s["consts"], 48)
            sp.dma_start(sorted_dram[SPARE:SPARE + BATCH, :].rearrange("(p r) c -> p r c", r=PARTS), fill_rows[:]).then_inc(s["filled"], 16)
            sp.wait_ge(s["memory"], 1)
            sp.dma_start(out[TOKENS:TOKENS + BATCH, :].rearrange("(p r) c -> p r c", r=PARTS), zero_rows[:]).then_inc(s["filled"], 16)
            sp.wait_ge(s["end_set"], 1)
            for e in range(EXPERTS):
                at = sp.value_load(end_i[0:1, e:e + 1], min_val=e * REGION, max_val=e * REGION + TOKENS)
                sp.dma_start(sorted_dram[bass.ds(at, BATCH), :].rearrange("(p r) c -> p r c", r=PARTS), fill_rows[:])\
                  .then_inc(s["filled"], 16)
            sp.wait_ge(s["filled"], 16 * (EXPERTS + 2))

        @block.gpsimd
        def _(pool):
            pool.memset(zero_rows[:], 0.0)
            pool.memset(b2f[:], 0.0)
            pool.memset(b2s[:], 0.0)
            pool.memset(two_rows[:], 0.0).then_inc(s["memory"], 1)
            for n, row in enumerate((0, 32)):
                pool.wait_ge(s["memory"], n + 1)
                pool.memset(two_rows[row:row + 1, :], 1.0).then_inc(s["memory"], 1)

        @block.scalar
        def _(act):
            def load(e):
                act.dma_start(stage1[e % 2][:], w1[e]).then_inc(s_stage[e % 2], 16)
                act.dma_start(stage2[e % 2][:], w2[e]).then_inc(s_stage[e % 2], 16)

            load(0)
            load(1)
            act.wait_ge(s["memory"], 1)
            for row in (0, 32):
                act.dma_start(b2f[row:row + 1], b2).then_inc(s["bias_in"], 16)
            act.dma_start(b1s[:], b1).then_inc(s["bias_in"], 16)
            for e in range(EXPERTS):
                act.wait_ge(s_stage[e % 2], 32 * (e // 2 + 1))
                act.mul(w1s[0][:, e], stage1[e % 2][:], WS)
                act.mul(w2s[0][:, e], stage2[e % 2][:], WS).then_inc(s["split_hi"], 1)
                if e + 2 < EXPERTS:
                    act.wait_ge(s["split_hi"], e + 1)
                    act.wait_ge(s["split_lo"], e + 1)
                    load(e + 2)
            act.wait_ge(s["bias_in"], 48)
            for row in (0, 32):
                ins = act.mul(b2s[row:row + 1], b2f[row:row + 1], WS)
            ins.then_inc(s["bias_hi"], 1)

        @block.vector
        def _(dve):
            steps = [0]

            def then(ins):
                steps[0] += 1
                ins.then_inc(s["step"], 1)
                dve.wait_ge(s["step"], steps[0])

            dve.tensor_copy(end_i[:], region_end[0:1, :]).then_inc(s["end_set"], 1)
            dve.wait_ge(s["consts"], 48)
            then(dve.tensor_tensor(count[:], region_end[0:1, :], base[:], ALU.subtract))
            then(dve.tensor_scalar(count_i[:], count[:], float(BATCH - 1), None, ALU.add))
            then(dve.tensor_scalar(count_i[:], count_i[:], BATCH.bit_length() - 1, None, ALU.logical_shift_right))
            then(dve.tensor_copy(count[:], count_i[:]))
            then(dve.memset(ends[:, 0:1], 0.0))
            for e in range(EXPERTS):
                then(dve.tensor_tensor(ends[:, e + 1:e + 2], ends[:, e:e + 1], count[:, e:e + 1], ALU.add))
            then(dve.scalar_tensor_tensor(out=first[:], in0=ends[:, 0:EXPERTS], scalar=-float(BATCH), in1=base[:], op0=ALU.mult, op1=ALU.add))
            then(dve.tensor_scalar(first[:], first[:], -float(SPARE), None, ALU.add))
            wide = number[:].unsqueeze(2).to_broadcast(MAP)
            then(dve.tensor_tensor(begun[:], wide, ends[:, 0:EXPERTS].unsqueeze(1).to_broadcast(MAP), ALU.is_ge))
            then(dve.tensor_tensor(passed[:], wide, ends[:, 1:EXPERTS + 1].unsqueeze(1).to_broadcast(MAP), ALU.is_ge))
            then(dve.tensor_reduce(sums[0][:], passed[:], AX.X, ALU.add))
            then(dve.tensor_scalar(batch_expert[:], sums[0][:], float(EXPERTS - 1), None, ALU.min))
            then(dve.tensor_tensor(begun[:], begun[:], passed[:], ALU.subtract))
            then(dve.tensor_reduce(sums[1][:], begun[:], AX.X, ALU.add))
            then(dve.tensor_tensor(begun[:], begun[:], first[:].unsqueeze(1).to_broadcast(MAP), ALU.mult))
            then(dve.tensor_reduce(sums[2][:], begun[:], AX.X, ALU.add))
            then(dve.tensor_tensor(sums[1][:], sums[1][:], number[:], ALU.mult))
            then(dve.scalar_tensor_tensor(out=sums[2][:], in0=sums[1][:], scalar=float(BATCH), in1=sums[2][:], op0=ALU.mult, op1=ALU.add))
            then(dve.tensor_scalar(batch_row[:], sums[2][:], float(SPARE), None, ALU.add))
            for e in range(EXPERTS):
                dve.wait_ge(s["split_hi"], e + 1)
                dve.scalar_tensor_tensor(out=w1s[1][:, e], in0=stage1[e % 2][:, 0:2, :], scalar=WS, in1=w1s[0][:, e, 0:2, :],
                                         op0=ALU.mult, op1=ALU.subtract)
                dve.scalar_tensor_tensor(out=w2s[1][:, e], in0=stage2[e % 2][:], scalar=WS, in1=w2s[0][:, e],
                                         op0=ALU.mult, op1=ALU.subtract).then_inc(s["split_lo"], 1)
            dve.wait_ge(s["bias_hi"], 1)
            dve.scalar_tensor_tensor(out=b2s[32:33], in0=b2f[32:33], scalar=WS, in1=b2s[32:33],
                                     op0=ALU.mult, op1=ALU.subtract)


def batch_pipeline(eng, body):
    for u in range(4):
        body(u, u, 0)
    with eng.Fori(1, BATCHES // 4) as p:
        for k in range(4):
            body(4 * p + k, k, p)
    for u in range(BATCHES - 2, BATCHES):
        body(u, u % 4, u // 4)


def experts_part(nc, sorted_dram, batch_row, batch_expert, ident16, w1s, w2s, b1s, b2s, two_rows, out):
    with ExitStack() as ctx:
        def sb(name, shape, dt):
            return ctx.enter_context(nc.sbuf_tensor(name, shape, dt))

        def pb(name, shape, dt):
            return ctx.enter_context(nc.psum_tensor(name, shape, dt))

        def sem(name):
            return ctx.enter_context(nc.semaphore(name))

        rows = [sb(f"rows{k}", [128, PARTS, PAYLOAD], U16) for k in range(4)]
        token = [sb(f"token{k}", [128, PARTS], U32) for k in range(4)]
        weight = [sb(f"weight{k}", [128, PARTS], F32) for k in range(4)]
        bias = [sb(f"bias{k}", [128, MF], F32) for k in range(2)]
        xT = [sb(f"e_xT{k}", [128, PARTS, 3, 128], F16) for k in range(2)]
        act_out = sb("act_out", [128, MF, BATCH], F32)
        g_hi = [sb(f"g_hi{k}", [128, MF, BATCH], F16) for k in range(2)]
        g_lo = [sb(f"g_lo{k}", [128, MF, BATCH], F16) for k in range(2)]
        y = [sb(f"y{k}", [128, PARTS, D], F32) for k in range(2)]
        carrier = sb("e_carrier", [32, 2], F32)
        up = [pb(f"up{k}", [128, BATCH], F32) for k in range(3)]
        down = pb("down", [128, 2, 512], F32)
        turned = pb("turned", [128, 2, 512], F32)
        s = {n: sem("e_" + n) for n in "turned xT_set up_done gelu_done hi_done lo_done down_done y_set meta_set memory carried".split()}
        s_rows = [sem(f"e_rows{k}") for k in range(4)]
        s_sent = [sem(f"e_sent{k}") for k in range(2)]
        SENT = 16 * PARTS
        block = ctx.enter_context(nc.Block())

        def last(u, back=0):
            return isinstance(u, int) and u >= BATCHES - 1 - back

        def expert_of(eng, u):
            at = batch_expert[0:1, u:u + 1] if isinstance(u, int) else batch_expert[0:1, bass.ds(u, 1)]
            return eng.value_load(at, min_val=0, max_val=EXPERTS - 1)

        @block.sync
        def _(sp):
            def load(u, k):
                at = batch_row[0:1, u:u + 1] if isinstance(u, int) else batch_row[0:1, bass.ds(u, 1)]
                row = sp.value_load(at, min_val=0, max_val=SPARE)
                sp.dma_start(rows[k][:], sorted_dram[bass.ds(row, BATCH), :].rearrange("(p r) c -> p r c", r=PARTS))\
                  .then_inc(s_rows[k], 16)

            load(0, 0)
            load(1, 1)

            def body(u, k, p):
                if not last(u, 1):
                    need(sp, s["turned"], u - 1)
                    need(sp, s["meta_set"], u - 1)
                    load(u + 2, (k + 2) % 4)

            batch_pipeline(sp, body)

        @block.gpsimd
        def _(pool):
            pool.memset(carrier[:], 0.0).then_inc(s["memory"], 1)
            pool.wait_ge(s["memory"], 1)

            def body(u, k, p):
                pool.wait_ge(s["y_set"], u + 1)
                need(pool, s_sent[1 - k % 2], SENT * (2 * p + (k + 1) // 2))
                need(pool, s["carried"], u)
                pool.tensor_tensor(carrier[:, 1:2], carrier[:, 0:1], carrier[:, 0:1], ALU.mult).then_inc(s["carried"], 1)
                for n in range(PARTS):
                    pool.indirect_dma_start(out=out, out_offset=bass.IndirectOffsetOnAxis(ap=token[k][:, n:n + 1], axis=0),
                                            in_=y[k % 2][:, n, :], in_offset=None, compute_op=ALU.add).then_inc(s_sent[k % 2], 16)

            batch_pipeline(pool, body)
            for k in range(2):
                pool.wait_ge(s_sent[k], SENT * BATCHES // 2)

        @block.scalar
        def _(act):
            def take(u, k):
                act.wait_ge(s["turned"], u + 1)
                need(act, s["up_done"], MF * (u - 1))
                act.copy(xT[k % 2][:].rearrange("p (b n) c r -> p b (n c r)", b=2), turned[:].bitcast(F16)[:, :, 0:6 * 128])\
                   .then_inc(s["xT_set"], 1)

            def gelu(u, k):
                act.wait_ge(s["meta_set"], u + 1)
                for m in range(MF):
                    act.wait_ge(s["up_done"], MF * u + m + 1)
                    need(act, s["lo_done"], MF // 2 * (u - 1) + m // 2 + 1)
                    act.activation(act_out[:, m, :], up[m % 3][:], ACT.Gelu, bias=bias[k % 2][:, m:m + 1], scale=1.0 / WS)\
                       .then_inc(s["gelu_done"], 1)

            take(0, 0)
            take(1, 1)
            gelu(0, 0)

            def body(u, k, p):
                if not last(u, 1):
                    take(u + 2, k + 2)
                if not last(u):
                    gelu(u + 1, k + 1)

            batch_pipeline(act, body)

        @block.vector
        def _(dve):
            def meta(u, k):
                e = expert_of(dve, u)
                dve.wait_ge(s_rows[k], 16 * (u // 4 + 1) if isinstance(u, int) else 4 * (u - k) + 16)
                need(dve, s["gelu_done"], MF * (u - 1))
                dve.tensor_scalar(bias[k % 2][:], b1s[:, bass.ds(e, 1), :].rearrange("p a m -> p (a m)"), 0.0, None, ALU.add)
                dve.tensor_scalar(weight[k][:], rows[k][:, :, WEIGHT_AT:PAYLOAD].bitcast(F32)[:, :, bass.ds(e, 1)].rearrange("p n a -> p (n a)"),
                                  0.0, None, ALU.add)
                dve.tensor_copy(token[k][:], rows[k][:, :, NUMBER_AT:WEIGHT_AT].bitcast(U32).rearrange("p n a -> p (n a)"))\
                   .then_inc(s["meta_set"], 1)

            def split(u, k):
                for j in range(MF // 2):
                    m = slice(2 * j, 2 * j + 2)
                    dve.wait_ge(s["gelu_done"], MF * u + 2 * j + 2)
                    need(dve, s["down_done"], u - 1)
                    dve.tensor_copy(g_hi[k % 2][:, m, :], act_out[:, m, :]).then_inc(s["hi_done"], 1)
                    dve.wait_ge(s["hi_done"], MF // 2 * u + j + 1)
                    dve.tensor_tensor(g_lo[k % 2][:, m, :], act_out[:, m, :], g_hi[k % 2][:, m, :], ALU.subtract).then_inc(s["lo_done"], 1)

            meta(0, 0)
            meta(1, 1)
            split(0, 0)

            def body(u, k, p):
                if not last(u):
                    split(u + 1, k + 1)
                need(dve, s_sent[k % 2], SENT * (2 * p + k // 2))
                if not last(u, 1):
                    meta(u + 2, (k + 2) % 4)
                dve.wait_ge(s["down_done"], u + 1)
                wide = [128, 2, 2, D]
                dve.tensor_tensor(y[k % 2][:].rearrange("p (b n) c -> p b n c", b=2), down[:, :, 0:2 * D].rearrange("p b (n c) -> p b n c", n=2),
                                  weight[k][:].rearrange("p (b n) -> p b n", b=2).unsqueeze(3).to_broadcast(wide), ALU.mult).then_inc(s["y_set"], 1)

            batch_pipeline(dve, body)

        @block.tensor
        def _(pe):
            def turn(u, k):
                pe.wait_ge(s_rows[k], 16 * (u // 4 + 1) if isinstance(u, int) else 4 * (u - k) + 16)
                need(pe, s["xT_set"], u)
                for n in range(PARTS):
                    for c in range(3):
                        at = (3 * (n % 2) + c) * 128
                        ins = pe.transpose(turned[:, n // 2, :].bitcast(F16)[:, at:at + 128], rows[k][:, n, 128 * c:128 * c + 128].bitcast(F16), ident16[:])
                ins.then_inc(s["turned"], 1)

            def up_product(u, k, e):
                pe.wait_ge(s["xT_set"], u + 1)
                for m in range(MF):
                    need(pe, s["gelu_done"], MF * u + m - 2)
                    for j, (c, w, h) in enumerate(PRODUCTS):
                        ins = pe.matmul(up[m % 3][:], w1s[h][:, bass.ds(e, 1), w, 128 * m:128 * m + 128].rearrange("p a c -> p (a c)"),
                                        xT[k % 2][:, :, c, :], start=(j == 0), stop=(j == len(PRODUCTS) - 1))
                    ins.then_inc(s["up_done"], 1)

            def down_product(u, k, e):
                pe.wait_ge(s["lo_done"], MF // 2 * (u + 1))
                need(pe, s["y_set"], u)
                for n in range(PARTS):
                    dst = down[:, n // 2, (n % 2) * D:(n % 2) * D + D]
                    pe.matmul(dst, two_rows[:], b2s[:, bass.ds(e, 1), :], start=True, stop=False)
                    cols = slice(128 * n, 128 * n + 128)
                    for m in range(MF):
                        high, low = (w2s[h][:, bass.ds(e, 1), m, :] for h in range(2))
                        pe.matmul(dst, g_hi[k % 2][:, m, cols], high, start=False, stop=False)
                        pe.matmul(dst, g_hi[k % 2][:, m, cols], low, start=False, stop=False)
                        ins = pe.matmul(dst, g_lo[k % 2][:, m, cols], high, start=False, stop=(m == MF - 1))
                ins.then_inc(s["down_done"], 1)

            turn(0, 0)
            turn(1, 1)
            up_product(0, 0, expert_of(pe, 0))

            def body(u, k, p):
                if not last(u, 1):
                    turn(u + 2, (k + 2) % 4)
                if not last(u):
                    up_product(u + 1, k + 1, expert_of(pe, u + 1))
                down_product(u, k, expert_of(pe, u))

            batch_pipeline(pe, body)


def lay_out(x, L0_tok_W, L0_tok_b, L0_tok_class_token, L0_tok_pos_embed, L0_attn_w_qkv, L0_attn_w_proj,
            L0_attn_b_proj, L0_ffn_router_w, L0_ffn_w1, L0_ffn_b1, L0_ffn_w2, L0_ffn_b2):
    f = np.float32
    patches = np.asarray(x).reshape(IMGS, CHANS, NPATCH, PATCH, NPATCH, PATCH).transpose(0, 1, 3, 5, 2, 4)
    patches = patches.reshape(IMGS, KIN, 128, SEQ - 1).transpose(0, 2, 1, 3)
    xt = np.zeros((IMGS, 128, KIN, SPAN), f)
    xt[..., 1:SEQ] = patches

    def two_tiles(a):
        a = np.concatenate([a, np.zeros((SPAN - SEQ, D), f)])
        return np.ascontiguousarray(a.reshape(2, ROWS, D).transpose(1, 0, 2))

    def stacked(w):
        return np.ascontiguousarray(np.asarray(w)[np.array(STACK)].transpose(1, 0, 2))

    bias_tab = np.concatenate([np.asarray(L0_tok_class_token), np.repeat(np.asarray(L0_tok_b)[None], SEQ - 1, 0)])
    qkv = np.asarray(L0_attn_w_qkv)
    cols = [which * D + (g * HPG + h) * DH + d for which in range(2) for g in range(GROUPS) for h in range(HPG)
            for _ in range(2) for d in range(DH)]
    r, c = np.arange(ROWS)[:, None], np.arange(KEYS)[None]
    band = np.stack([np.where((abs((c + KEYS_AT[n]) - (r + n * ROWS)) <= HALF_WIN) & (c + KEYS_AT[n] < SEQ), 0.0, MASKED)
                     for n in range(2)], 1)
    fill = np.zeros((128, PARTS, PAYLOAD), np.uint16)
    fill[:, :, NUMBER_AT:WEIGHT_AT] = (TOKENS + np.arange(BATCH, dtype=np.uint32)).reshape(128, PARTS, 1).view(np.uint16)
    return {
        "xt": xt,
        "w_embed": np.asarray(L0_tok_W).T.reshape(KIN, 128, D).transpose(1, 0, 2),
        "bias_tab": two_tiles(bias_tab),
        "pos": two_tiles(np.asarray(L0_tok_pos_embed)),
        "w_qk": stacked(qkv[:, cols]),
        "w_v": stacked(qkv[:, 2 * D:]),
        "w_p": stacked(L0_attn_w_proj),
        "b_p": np.asarray(L0_attn_b_proj)[None],
        "router": stacked(np.asarray(L0_ffn_router_w).T),
        "w1": np.stack([stacked(w) for w in np.asarray(L0_ffn_w1)]),
        "b1": np.asarray(L0_ffn_b1).reshape(EXPERTS, MF, 128).transpose(2, 0, 1),
        "w2": np.asarray(L0_ffn_w2).reshape(EXPERTS, MF, 128, D).transpose(0, 2, 1, 3),
        "b2": np.asarray(L0_ffn_b2).reshape(1, EXPERTS, D),
        "ident": np.eye(128, dtype=f),
        "above": np.triu(np.ones((128, 128), f), 1),
        "numbers": np.arange(BATCHES, dtype=f)[None],
        "token_no": (np.arange(ROWS)[:, None, None] + ROWS * np.arange(2)[None, None] + SEQ * np.arange(IMGS)[None, :, None]).astype(f),
        "fill": fill,
        "region_at": np.repeat(REGION * np.arange(EXPERTS, dtype=f)[None], 128, 0),
        "band": band.astype(f),
        "low_rows": -(np.arange(128) % 32 >= DH).astype(f)[:, None],
    }


def kernel(**inputs):
    import concourse.bacc as bacc
    from concourse.bass_utils import run_bass_kernel_spmd

    nc = bacc.Bacc("TRN2", target_bir_lowering=False, num_devices=1)
    arrays, args = {}, {}
    for name, a in lay_out(**inputs).items():
        a = np.ascontiguousarray(a)
        arrays[f"in_{name}"] = a
        args[name] = nc.dram_tensor(f"in_{name}", a.shape, mybir.dt.from_np(a.dtype), kind="ExternalInput").ap()
    args["out"] = nc.dram_tensor("out_0", (TOKENS + BATCH, D), F32, kind="ExternalOutput").ap()
    vit_tower(nc, **args)
    result = run_bass_kernel_spmd(nc, [arrays], core_ids=[0])
    return result.results[0]["out_0"][:TOKENS].reshape(IMGS, SEQ, D)
```

```python
from contextlib import ExitStack

import numpy as np

import concourse.bass as bass
from concourse import mybir

F32 = mybir.dt.float32
F16 = mybir.dt.float16
BF16 = mybir.dt.bfloat16
U16 = mybir.dt.uint16
U32 = mybir.dt.uint32
I32 = mybir.dt.int32
ALU = mybir.AluOpType
ACT = mybir.ActivationFunctionType
AX = mybir.AxisListType

IMGS, CHANS, SIDE, NPATCH = 64, 3, 224, 14
PATCH = SIDE // NPATCH
SEQ = NPATCH * NPATCH + 1
D = 192
DIN = CHANS * PATCH * PATCH
KIN = DIN // 128
HEADS, DH = 12, 16
GROUPS = 3
HPG = HEADS // GROUPS
REACH = 6
WINDOWS, QUERIES, KEYS = 4, 50, 64
ROWS = 2 * QUERIES
SPAN = 2 * ROWS
PITCH = ROWS + ROWS % 2
TILE_ROWS = (ROWS, SEQ - ROWS)
WIDTH = (WINDOWS - 1) * QUERIES + REACH + KEYS
assert SPAN >= SEQ and QUERIES + 2 * REACH <= KEYS
EXPERTS, FF = 8, 768
MF = FF // 128
WS = 64.0
EPS = 1e-5
MASKED = -1e30
CHOSEN = 2
TOKENS = IMGS * SEQ
NUMBER_AT = 2 * D
WEIGHT_AT = NUMBER_AT + 2
PAYLOAD = WEIGHT_AT + 2 * EXPERTS
BATCH = 512
PARTS = BATCH // 128
REGION = TOKENS + BATCH
SPARE = EXPERTS * REGION
BATCHES = (CHOSEN * TOKENS + EXPERTS * (BATCH - 1)) // BATCH
BATCHES += (2 - BATCHES) % 4
STEPS, COUNTS_READ = 25, 13
PART_AT = (0, 5, 11, COUNTS_READ, STEPS)

STACK = [list(range(128)), list(range(128, 192)) + list(range(64)), list(range(64, 192))]
PRODUCTS = [(0, 0, 0), (1, 1, 0), (2, 2, 0), (0, 0, 1), (1, 1, 1)]


def need(eng, sem, value):
    if not isinstance(value, int) or value > 0:
        eng.wait_ge(sem, value)


def need_apart(eng, sem, value, met):
    eng.wait_ge(*met)
    eng.wait_ge(sem, value)


def pipeline(eng, body):
    for t in range(8):
        body(t, t % 4, t // 4)
    with eng.Fori(2, IMGS // 4) as p:
        for k in range(4):
            body(4 * p + k, k, p)
    for t in range(IMGS, IMGS + 8):
        body(t, t % 4, t // 4)


def runs(t, behind):
    return not isinstance(t, int) or behind <= t < IMGS + behind


def images(n):
    return min(n, IMGS) if isinstance(n, int) else n


def groups(t, k, p, behind):
    return 2 * p + (k - behind) // 2, (k - behind) % 2 == 0 and runs(t, behind)


EARLY = 4


def expert_loaded(t):
    if isinstance(t, int):
        if 1 <= t <= EARLY:
            return t - 1
        if IMGS <= t < IMGS + EXPERTS - EARLY:
            return t - IMGS + EARLY
    return None


def vit_tower(nc, xt, w_embed, bias_tab, pos, w_qk, w_v, w_p, b_p, router, w1, b1, w2, b2,
              ident, band, low_rows, above, numbers, token_no, fill, region_at, out):
    sorted_dram = nc.dram_tensor("sorted_scratch", (SPARE + BATCH, PAYLOAD), U16).ap()
    with ExitStack() as ctx:
        def sb(name, shape, dt):
            return ctx.enter_context(nc.sbuf_tensor(name, shape, dt))

        ident16 = sb("ident16", [128, 128], F16)
        w1s = [sb("w1_hi", [128, EXPERTS, 3, FF], F16), sb("w1_lo", [128, EXPERTS, 2, FF], F16)]
        w2s = [sb("w2_hi", [128, EXPERTS, MF, D], F16), sb("w2_lo", [128, EXPERTS, MF, D], F16)]
        b1s = sb("b1s", [128, EXPERTS, MF], F32)
        ones16 = sb("ones16", [128, 128], F16)
        batch_row = sb("batch_row", [1, BATCHES], I32)
        batch_expert = sb("batch_expert", [1, BATCHES], I32)
        attention_part(nc, xt, w_embed, bias_tab, pos, w_qk, w_v, w_p, b_p, router, w1, w2, b1, ident, band, low_rows,
                       above, token_no, region_at, numbers, fill, ident16, w1s, w2s, b1s, ones16,
                       batch_row, batch_expert, sorted_dram, out)
        experts_part(nc, sorted_dram, batch_row, batch_expert, ident16, w1s, w2s, b1s, b2, out)


def attention_part(nc, xt, w_embed, bias_tab, pos, w_qk, w_v, w_p, b_p, router, w1, w2, b1, ident, band, low_rows,
                   above, token_no, region_at, numbers, fill, ident16, w1s, w2s, b1s, ones16,
                   batch_row, batch_expert, sorted_dram, out):
    with ExitStack() as ctx:
        def sb(name, shape, dt):
            return ctx.enter_context(nc.sbuf_tensor(name, shape, dt))

        def pb(name, shape, dt):
            return ctx.enter_context(nc.psum_tensor(name, shape, dt))

        def sem(name):
            return ctx.enter_context(nc.semaphore(name))

        identf = sb("identf", [128, 128], F32)
        identb = sb("identb", [128, 128], BF16)
        above16 = sb("above16", [128, 128], F16)
        rank = sb("rank", [ROWS, EXPERTS], F32)
        tokens = sb("tokens", [ROWS, IMGS, 2], mybir.dt.int16)
        bandb = sb("bandb", [128, 2, KEYS], BF16)
        low = sb("low", [128, 1], F32)
        we = sb("we", [128, KIN, D], F32)
        tab = sb("tab", [ROWS, 2, D], F32)
        stage1 = sb("stage1", [128, 3, FF], F32)
        stage2 = sb("stage2", [128, MF, D], F32)
        weights32, weights16 = {"wqk": stage1[:], "wv": stage2[:, 0:3, :], "wp": stage2[:, 3:6, :]}, {}
        weights32["wr"] = sb("wr32", [128, 3, EXPERTS], F32)[:]
        for name, cols in (("wqk", 2 * GROUPS * 128), ("wv", D), ("wp", D), ("wr", EXPERTS)):
            weights16[name] = [sb(name + "_hi", [128, 3, cols], F16), sb(name + "_lo", [128, 2, cols], F16)]
        wqk, wv, wp, wr = weights16.values()
        bp = sb("bp", [128, D], F16)
        carrier = sb("carrier", [32, 2], F32)
        half_pow = sb("half_pow", [128, 2], F32)
        eps = sb("eps", [128, 2], F32)

        MAP = [1, BATCHES, EXPERTS]
        region_end = [sb(f"region_end{k}", [128, EXPERTS], F32) for k in range(2)]


        patches = [sb(f"patches{k}", [128, KIN, SPAN], F32) for k in range(2)]
        fill_rows = patches[0][:].rearrange("p a n -> p (a n)")[:, 0:PARTS * PAYLOAD // 2].bitcast(U16).rearrange("p (r c) -> p r c", r=PARTS)
        zero_rows = patches[1][:].rearrange("p a n -> p (a n)")[:, 0:PARTS * D]
        h1 = [sb(f"h1_{k}", [ROWS, 2, D], F32) for k in range(4)]
        st1 = sb("st1", [ROWS, 2, 6], F32)
        mv1 = sb("mv1", [ROWS, 2, 2], F32)
        rs1 = sb("rs1", [ROWS, 2], F32)
        xn1 = sb("xn1", [ROWS, 2, D], F32)
        post = xn1
        xs1 = sb("xs1", [ROWS, 2, 2 * D], F16)
        xT1 = sb("xT1", [128, 3, WIDTH], F16)
        xV = sb("xV", [128, 3, WINDOWS, 2, KEYS], F16)
        qk_hi = sb("qk_hi", [128, GROUPS, 2, WIDTH], F16)
        q_lo = sb("q_lo", [128, GROUPS, WIDTH], F16)
        k_st = sb("k_st", [128, GROUPS, SPAN], F16)
        k_diag = sb("k_diag", [128, GROUPS, HPG, WIDTH], F16)

        v_hi = [sb(f"v_hi{k}", [128, WINDOWS, HEADS // 2, 2 * (DH + 1)], F16) for k in range(4)]
        v_lo = [sb(f"v_lo{k}", [128, WINDOWS, HEADS // 2, 2 * (DH + 1)], F16) for k in range(4)]
        prob = sb("prob", [128, 2 * HEADS, KEYS], F32)
        flat = prob[:].rearrange("p h c -> p (h c)")
        above32, bandf = flat[:, 0:128], flat[:, 128:128 + 2 * KEYS].rearrange("p (n c) -> p n c", n=2)
        bp32 = flat[0:64, 256:256 + D]
        table_sizes = [BATCHES * EXPERTS] * 2 + [BATCHES] * 4 + [EXPERTS] * 4 + [EXPERTS + 1, EXPERTS]
        tables = [flat[0:1, sum(table_sizes[:n]):sum(table_sizes[:n + 1])] for n in range(len(table_sizes))]
        begun, passed = (a.rearrange("p (b e) -> p b e", e=EXPERTS) for a in tables[0:2])
        sums, number, base, count, ends, first = tables[2:5], tables[5], tables[6], tables[7], tables[10], tables[11]
        count_i, end_i = (a.bitcast(I32) for a in tables[8:10])
        mx = sb("mx", [128, 2 * HEADS], F32)
        pT_hi = sb("pT_hi", [128, HEADS, 128], F16)
        pT_lo = sb("pT_lo", [128, HEADS, 128], F16)
        rden = sb("rden", [128, 2, HEADS], F32)
        on = sb("on", [128, 2, D], F32)
        os_ = sb("os", [128, 2, 2 * D], F16)

        oT = sb("oT", [128, 2, 3, ROWS], F16)
        h2 = sb("h2", [ROWS, 2, D], F32)
        st2 = sb("st2", [ROWS, 2, 6], F32)
        mv2 = sb("mv2", [ROWS, 2, 2], F32)
        rs2 = sb("rs2", [ROWS, 2], F32)
        xn2 = sb("xn2", [ROWS, 2, D], F32)
        xT2 = sb("xT2", [128, 2, 3, ROWS], F16)
        payload = sb("payload", [ROWS, 8, PAYLOAD], U16)

        T8 = [ROWS, 4, EXPERTS]
        logit = sb("logit", T8, F32)
        chosen = [sb(f"chosen{k}", T8, F32) for k in range(CHOSEN)]
        scaled = [sb(f"scaled{k}", T8, F32) for k in range(CHOSEN)]
        tmp = sb("tmp", T8, F32)
        marks = sb("marks", T8, F16)
        top, best, second, ratio = (sb(n, [ROWS, 4], F32) for n in ("top", "best", "second", "ratio"))
        place_f = sb("place_f", [ROWS, 4, CHOSEN], F32)
        place = [sb(f"place{k}", [ROWS, 4, CHOSEN], U32) for k in range(2)]

        scores = pb("scores", [128, 3, 512], F32)
        wide = pb("wide", [128, 3, 512], F32)
        near = pb("near", [128, 512], F32)
        far = pb("far", [128, 512], F32)

        names = ("first_in tab_set load_c zero_mem weights embedded h1_set stats1 aggr1 rstd1 normed1 hi1 lo1 turned1 xT_set xV_set qk_done "
                 "qk_hi_set q_lo_set k_st_set k_diag_set v_done v_hi_set v_lo_set norm_done o_hi_set "
                 "max_set scored shifted exp_set prob_turned p_hi_set p_lo_set "
                 "o_lo_set o_turned oT_set proj_done h2_set stats2 aggr2 rstd2 normed2 hi2 lo2 den_set "
                 "pv_done var1 var2 setup1 setup2 turned2 xT2_set routed logit_set step weighed marks_set counted carried staged split_hi split_lo h2_out "
                 "later_in filled end_set table_step").split()
        s = {n: sem(n) for n in names}
        s_patch = [sem(f"patches_in{k}") for k in range(2)]
        s_sent = [sem(f"sent{k}") for k in range(4)]
        SENT = 16 * 2 * CHOSEN

        def value_halves(v, half):
            q, col = slice(64 * half, 64 * half + 64), half * (DH + 1)
            to = v[q, :, :, col:col + DH].rearrange("p (b w) h d -> p b (w h) d", b=2)
            product = scores[q, 0:2, 0:2 * D].rearrange("p b (m x d) -> p b m x d", x=2, d=DH)[:, :, :, half, :]
            return to, product

        block = ctx.enter_context(nc.Block())

        @block.sync
        def _(sp):
            for dst, src in ((we[:], w_embed), (tab[:], bias_tab), (post[:], pos)):
                sp.dma_start(dst, src).then_inc(s["first_in"], 16)
            sp.dma_start(patches[0][:], xt[0:1].rearrange("a p k n -> p (a k) n")).then_inc(s_patch[0], 16)
            for dst, src in ((identf[:], ident), (bandf, band),
                             (low[:], low_rows), (weights32["wqk"], w_qk), (weights32["wv"], w_v),
                             (weights32["wp"], w_p), (weights32["wr"], router), (above32, above), (tokens[:], token_no)):
                sp.dma_start(dst, src).then_inc(s["load_c"], 16)
            sp.dma_start(region_end[0][:], region_at).then_inc(s["load_c"], 16)
            sp.wait_ge(s["zero_mem"], 1)
            for n, row in enumerate((0, 32)):
                sp.dma_start(bp32[row:row + 1, :], b_p).then_inc(s["setup1"], 16)

            def body(t, k, p):
                if runs(t, 0) and not (isinstance(t, int) and t == 0):
                    need(sp, s["embedded"], t - 1)
                    src = xt[t:t + 1] if isinstance(t, int) else xt[bass.ds(t, 1)]
                    sp.dma_start(patches[k % 2][:], src.rearrange("a p k n -> p (a k) n")).then_inc(s_patch[k % 2], 16)
                if runs(t, 1):
                    g = t - 1
                    sp.wait_ge(s["k_st_set"], g + 1)
                    for h in range(HPG):
                        q = slice(32 * h, 32 * h + 32)
                        sp.dma_start(k_diag[q, :, h, REACH:REACH + SPAN], k_st[q, :, :]).then_inc(s["k_diag_set"], 16)
                if isinstance(t, int) and t == EARLY + 1:
                    sp.dma_start(b1s[:], b1).then_inc(s["later_in"], 16)
                if isinstance(t, int) and t == IMGS + 2:
                    sp.wait_ge(s["embedded"], IMGS)
                    sp.dma_start(fill_rows, fill).then_inc(s["later_in"], 16)
                if isinstance(t, int) and t == IMGS + 3:
                    sp.wait_ge(s["prob_turned"], GROUPS * IMGS)
                    sp.dma_start(number, numbers).then_inc(s["later_in"], 16)
                    sp.dma_start(base, region_at[0:1, :]).then_inc(s["later_in"], 16)

            pipeline(sp, body)
            sp.wait_ge(s["zero_mem"], 4)
            sp.dma_start(out[TOKENS:TOKENS + BATCH, :].rearrange("(p r) c -> p (r c)", r=PARTS), zero_rows).then_inc(s["filled"], 16)
            sp.wait_ge(s["later_in"], 64)
            sp.dma_start(sorted_dram[SPARE:SPARE + BATCH, :].rearrange("(p r) c -> p r c", r=PARTS), fill_rows).then_inc(s["filled"], 16)
            sp.wait_ge(s["end_set"], 1)
            for e in range(EXPERTS):
                at = sp.value_load(end_i[0:1, e:e + 1], min_val=e * REGION, max_val=e * REGION + TOKENS)
                sp.dma_start(sorted_dram[bass.ds(at, BATCH), :].rearrange("(p r) c -> p r c", r=PARTS), fill_rows)\
                  .then_inc(s["filled"], 16)
            sp.wait_ge(s["filled"], 16 * (EXPERTS + 2))

        @block.gpsimd
        def _(pool):
            pool.memset(bp32[:], 0.0)
            pool.memset(bp[:], 0.0)
            pool.memset(ones16[:], 1.0)
            pool.memset(half_pow[:], -0.5)
            pool.memset(eps[:], EPS)
            pool.memset(carrier[:], 0.0).then_inc(s["carried"], 1)
            for a in (xT1, qk_hi, q_lo, *v_hi, *v_lo):
                pool.memset(a[:], 0.0)
            for e in range(EXPERTS):
                pool.memset(rank[:, e:e + 1], float(EXPERTS - e))
            pool.memset(k_diag[:], 0.0).then_inc(s["zero_mem"], 1)
            pool.wait_ge(s["zero_mem"], 1)
            done = 1
            for half in range(2):
                for v in v_hi:
                    col = half * (DH + 1) + DH
                    ins = pool.memset(v[64 * half:64 * half + 64, :, :, col:col + 1], WS)
                ins.then_inc(s["zero_mem"], 1)
                done += 1
                pool.wait_ge(s["zero_mem"], done)

            def rsqrt(n_th, mv, rs, aggr, var, rstd, read):
                pool.wait_ge(s[aggr], n_th)
                pool.tensor_tensor(mv[:, :, 1], mv[:, :, 1], eps[0:ROWS, :], ALU.add).then_inc(s[var], 1)
                pool.wait_ge(s[var], n_th)
                need(pool, s[read], n_th - 1)
                pool.tensor_tensor(rs[:], mv[:, :, 1], half_pow[0:ROWS, :], ALU.pow).then_inc(s[rstd], 1)

            def body(t, k, p):
                f, c, b = t, t - 3, t - 4
                grp, gk = 2 * p - 4 + k // 2, k // 2
                if runs(t, 8):
                    pool.wait_ge(s["step"], STEPS * (grp + 1))
                    pool.wait_ge(s["carried"], t - 7)
                    pool.tensor_tensor(carrier[:, 1:2], carrier[:, 0:1], carrier[:, 0:1], ALU.mult).then_inc(s["carried"], 1)
                    for n in range(2):
                        rows = TILE_ROWS[n]
                        for j in range(CHOSEN):
                            at = place[gk][0:rows, 2 * (k % 2) + n, j:j + 1]
                            pool.indirect_dma_start(out=sorted_dram, out_offset=bass.IndirectOffsetOnAxis(ap=at, axis=0),
                                                    in_=payload[0:rows, 2 * k + n, :], in_offset=None).then_inc(s_sent[k], 16)
                if runs(t, 4):
                    rsqrt(b + 1, mv2, rs2, "aggr2", "var2", "rstd2", "normed2")
                if runs(t, 4):
                    pool.wait_ge(s["hi2"], b + 1)
                    dst = payload[:, 2 * k:2 * k + 2, :].bitcast(F16)
                    pool.tensor_tensor(dst[:, :, D:2 * D], xn2[:], dst[:, :, 0:D], ALU.subtract).then_inc(s["lo2"], 1)
                if isinstance(t, int) and t == IMGS + 2:
                    pool.wait_ge(s["embedded"], IMGS)
                    pool.memset(zero_rows, 0.0).then_inc(s["zero_mem"], 1)
                if runs(t, 0):
                    rsqrt(f + 1, mv1, rs1, "aggr1", "var1", "rstd1", "normed1")
                if runs(t, 0):
                    pool.wait_ge(s["hi1"], f + 1)
                    need(pool, s["turned1"], f)
                    pool.tensor_tensor(xs1[:, :, D:], xn1[:], xs1[:, :, 0:D], ALU.subtract).then_inc(s["lo1"], 1)
                if runs(t, 3):
                    pool.wait_ge(s["o_hi_set"], c + 1)
                    pool.tensor_tensor(os_[:, :, D:], on[:], os_[:, :, 0:D], ALU.subtract).then_inc(s["o_lo_set"], 1)

            pipeline(pool, body)
            for k in range(4):
                pool.wait_ge(s_sent[k], SENT * IMGS // 4)

        @block.scalar
        def _(act):
            act.wait_ge(s["load_c"], 16 * 10)
            act.copy(ident16[:], identf[:])
            act.copy(identb[:], identf[:])
            act.copy(above16[:], above32)
            act.copy(bandb[:], bandf).then_inc(s["setup2"], 1)
            for name, w in weights32.items():
                act.mul(weights16[name][0][:], w, WS).then_inc(s["weights"], 1)
            act.wait_ge(s["setup1"], 32)
            for row in (0, 32):
                act.mul(bp[row:row + 1, :], bp32[row:row + 1, :], WS).then_inc(s["weights"], 1)

            def pieces(bank):
                return bank[:].bitcast(F16)[:, 0:6 * PITCH].rearrange("p (n c r) -> p n c r", n=2, c=3)[:, :, :, 0:ROWS]

            def body(t, k, p):
                f, g, a, c, b, r = (t - n for n in range(6))
                if runs(t, 3):
                    need(act, s["pv_done"], c)
                    for j in range(GROUPS):
                        act.wait_ge(s["prob_turned"], GROUPS * c + j + 1)
                        act.copy(pT_hi[:, 4 * j:4 * j + 4, :].rearrange("p m q -> p (m q)"), wide[:, j, :]).then_inc(s["p_hi_set"], 1)
                if runs(t, 1):
                    act.wait_ge(s["turned1"], g + 1)
                    need(act, s["qk_done"], g)
                    need(act, s["xV_set"], g)
                    act.copy(xT1[:, :, REACH:REACH + SPAN].rearrange("p c (n r) -> p n c r", n=2), pieces(near)).then_inc(s["xT_set"], 1)
                if runs(t, 5):
                    act.wait_ge(s["routed"], r + 1)
                    if k % 2:
                        need(act, s["marks_set"], groups(t, k, p, 5)[0])
                    slot = 2 * ((k - 5) % 2)
                    act.mul(logit[:, slot:slot + 2, :], far[0:ROWS, 0:2 * EXPERTS].rearrange("p (n e) -> p n e", n=2), 1.0 / WS)\
                       .then_inc(s["logit_set"], 1)
                if runs(t, 4):
                    act.wait_ge(s["o_turned"], b + 1)
                    need(act, s["proj_done"], b)
                    act.copy(oT[:].rearrange("p n c (x r) -> p (n c) x r", x=2),
                             far[:].bitcast(F16)[:, 0:6 * 128].rearrange("p (m x r) -> p m x r", m=6, x=2)[:, :, :, 0:QUERIES]).then_inc(s["oT_set"], 1)
                e = expert_loaded(t)
                if e is not None:
                    if e == 0:
                        act.wait_ge(s["setup2"], 2)
                    need(act, s["split_lo"], e)
                    act.dma_start(stage1[:], w1[e]).then_inc(s["staged"], 16)
                    act.dma_start(stage2[:], w2[e]).then_inc(s["staged"], 16)
                if runs(t, 1):
                    act.wait_ge(s["qk_done"], g + 1)
                    act.copy(qk_hi[:, :, :, REACH:REACH + SPAN], wide[:, :, 0:2 * SPAN].rearrange("p g (w n) -> p g w n", w=2)).then_inc(s["qk_hi_set"], 1)
                if runs(t, 2):
                    act.wait_ge(s["shifted"], GROUPS * (a + 1))
                    act.activation(prob[:], prob[:], ACT.Exp, scale=DH ** -0.5 / (WS * WS)).then_inc(s["exp_set"], 1)
                if runs(t, 4):
                    act.wait_ge(s["h2_set"], b + 1)
                    for n in range(2):
                        at, rows = b * SEQ + ROWS * n, TILE_ROWS[n]
                        d = out[at:at + rows, :] if isinstance(at, int) else out[bass.ds(at, rows), :]
                        act.dma_start(d, h2[0:rows, n, :]).then_inc(s["h2_out"], 16)
                    act.wait_ge(s["normed2"], b + 1)
                    need(act, s_sent[k], SENT * (p - 1))
                    act.copy(payload[:, 2 * k:2 * k + 2, 0:D].bitcast(F16), xn2[:]).then_inc(s["hi2"], 1)
                if runs(t, 1):
                    act.wait_ge(s["v_done"], g + 1)
                    need(act, s["pv_done"], g - 3)
                    for half in range(2):
                        v, src = value_halves(v_hi[(k - 1) % 4], half)
                        ins = act.copy(v, src)
                    ins.then_inc(s["v_hi_set"], 1)
                if e is not None:
                    act.wait_ge(s["staged"], 32 * (e + 1))
                    act.mul(w1s[0][:, e], stage1[:], WS)
                    act.mul(w2s[0][:, e], stage2[:], WS).then_inc(s["split_hi"], 1)
                if runs(t, 0):
                    act.wait_ge(s["normed1"], f + 1)
                    need(act, s["turned1"], f)
                    act.copy(xs1[:, :, 0:D], xn1[:]).then_inc(s["hi1"], 1)
                if runs(t, 4):
                    act.wait_ge(s["turned2"], b + 1)
                    need(act, s["routed"], b)
                    act.copy(xT2[:].rearrange("p n c r -> p (n c) r"), pieces(near).rearrange("p n c r -> p (n c) r")).then_inc(s["xT2_set"], 1)
                grp, due = groups(t, k, p, 6)
                if runs(t, 3):
                    act.wait_ge(s["norm_done"], c + 1)
                    need(act, s["o_turned"], c)
                    act.copy(os_[:, :, 0:D], on[:]).then_inc(s["o_hi_set"], 1)
                if due:
                    act.wait_ge(s["step"], STEPS * grp + PART_AT[1] + 2)
                    act.activation(ratio[:], second[:], ACT.Exp).then_inc(s["weighed"], 1)

            pipeline(act, body)
            act.wait_ge(s["h2_out"], 32 * IMGS)

        @block.vector
        def _(dve):
            dve.wait_ge(s["first_in"], 48)
            dve.tensor_tensor(tab[:], tab[:], post[:], ALU.add).then_inc(s["tab_set"], 1)
            dve.wait_ge(s["tab_set"], 1)

            def normalise(mv, rs, xn, h):
                for n in range(2):
                    ins = dve.tensor_scalar(xn[:, n, :], h[:, n, :], mv[:, n, 0:1], rs[:, n:n + 1], ALU.subtract, ALU.mult)
                return ins

            def statistics(h, st, mv, stats, aggr, n_th):
                for n in range(2):
                    ins = dve.bn_stats(st[:, n, :], h[:, n, :])
                ins.then_inc(stats, 1)
                need_apart(dve, stats, n_th, (s["first_in"], 48))
                for n in range(2):
                    ins = dve.bn_aggr(mv[:, n, :], st[:, n, :])
                ins.then_inc(aggr, 1)

            def over_experts(x):
                return x[:].unsqueeze(2).to_broadcast(T8)

            def route_steps(grp, gk, part):
                count = [PART_AT[part]]

                def then(ins):
                    count[0] += 1
                    ins.then_inc(s["step"], 1)
                    dve.wait_ge(s["step"], STEPS * grp + count[0])

                def choose(j):
                    then(dve.tensor_reduce(best[:], tmp[:], AX.X, ALU.max))
                    then(dve.tensor_tensor(chosen[j][:], tmp[:], over_experts(best), ALU.is_equal))

                ranks = rank[:].unsqueeze(1).to_broadcast(T8)
                if part == 0:
                    dve.wait_ge(s["logit_set"], 2 * grp + 2)
                    then(dve.tensor_reduce(top[:], logit[:], AX.X, ALU.max))
                    then(dve.tensor_tensor(logit[:], logit[:], over_experts(top), ALU.subtract))
                    then(dve.scalar_tensor_tensor(out=tmp[:], in0=logit[:], scalar=0.0, in1=ranks, op0=ALU.is_ge, op1=ALU.mult))
                    choose(0)
                if part == 1:
                    then(dve.scalar_tensor_tensor(out=logit[:], in0=chosen[0][:], scalar=MASKED, in1=logit[:], op0=ALU.mult, op1=ALU.add))
                    then(dve.tensor_reduce(second[:], logit[:], AX.X, ALU.max))
                    then(dve.tensor_tensor(tmp[:], logit[:], over_experts(second), ALU.is_ge))
                    then(dve.tensor_tensor(tmp[:], tmp[:], ranks, ALU.mult))
                    choose(1)
                    dve.tensor_tensor(marks[:], chosen[0][:], chosen[1][:], ALU.add).then_inc(s["marks_set"], 1)
                if part == 2:
                    dve.wait_ge(s["counted"], grp + 1)
                    counts = scores[0:ROWS, 2, 0:5 * EXPERTS].rearrange("p (n e) -> p n e", e=EXPERTS)
                    old, new = region_end[gk], region_end[1 - gk]
                    then(dve.tensor_tensor(tmp[:], counts[:, 0:4, :], old[0:ROWS, :].unsqueeze(1).to_broadcast(T8), ALU.add))
                    then(dve.tensor_tensor(new[0:ROWS, :], counts[:, 4, :], old[0:ROWS, :], ALU.add))
                if part == 3:
                    for j in range(CHOSEN):
                        then(dve.tensor_tensor(scaled[j][:], chosen[j][:], tmp[:], ALU.mult))
                        then(dve.tensor_reduce(place_f[:, :, j], scaled[j][:], AX.X, ALU.add))
                    then(dve.tensor_scalar(place[gk][:], place_f[:], 0.0, None, ALU.add))
                    dve.wait_ge(s["weighed"], grp + 1)
                    then(dve.tensor_scalar(best[:], ratio[:], 1.0, None, ALU.add))
                    then(dve.reciprocal(best[:], best[:]))
                    then(dve.tensor_tensor(ratio[:], ratio[:], best[:], ALU.mult))
                    for j, share in enumerate((best, ratio)):
                        then(dve.scalar_tensor_tensor(out=scaled[j][:], in0=chosen[j][:], scalar=1.0 / WS, in1=over_experts(share),
                                                      op0=ALU.mult, op1=ALU.mult))
                    mine = payload[:, 4 * gk:4 * gk + 4, :]
                    then(dve.tensor_tensor(mine[:, :, WEIGHT_AT:PAYLOAD].bitcast(F32), scaled[0][:], scaled[1][:], ALU.add))
                    img = tokens[:, 2 * grp:2 * grp + 2, :] if isinstance(grp, int) else tokens[:, bass.ds(2 * grp, 2), :]
                    then(dve.tensor_scalar(mine[:, :, NUMBER_AT:WEIGHT_AT].bitcast(U32).rearrange("p (i n) c -> p i (n c)", i=2),
                                           img, 0.0, None, ALU.add))
                assert count[0] == PART_AT[part + 1], count[0]

            def body(t, k, p):
                f, g, a, c, b, r = (t - n for n in range(6))
                if runs(t, 3):
                    need(dve, s["pv_done"], c)
                    for j in range(GROUPS):
                        dve.wait_ge(s["p_hi_set"], GROUPS * c + j + 1)
                        m = slice(4 * j, 4 * j + 4)
                        dve.tensor_tensor(pT_lo[:, m, :].rearrange("p m q -> p (m q)"), wide[:, j, :],
                                          pT_hi[:, m, :].rearrange("p m q -> p (m q)"), ALU.subtract).then_inc(s["p_lo_set"], 1)
                if runs(t, 1):
                    dve.wait_ge(s["xT_set"], g + 1)
                    need(dve, s["v_done"], g)
                    for i in range(WINDOWS):
                        src = xT1[:, :, QUERIES * i:QUERIES * i + KEYS].unsqueeze(2).to_broadcast([128, 3, 2, KEYS])
                        ins = dve.tensor_copy(xV[:, :, i], src)
                    ins.then_inc(s["xV_set"], 1)
                if runs(t, 2):
                    for j in range(GROUPS):
                        dve.wait_ge(s["scored"], GROUPS * a + j + 1)
                        dve.tensor_reduce(mx[:, 8 * j:8 * j + 8], scores[:, j, :].rearrange("p (h c) -> p h c", c=KEYS), AX.X, ALU.max)\
                           .then_inc(s["max_set"], 1)
                    need(dve, s["prob_turned"], GROUPS * a)
                    for j in range(GROUPS):
                        dve.wait_ge(s["max_set"], GROUPS * a + j + 1)
                        dve.tensor_tensor(prob[:, 8 * j:8 * j + 8, :], scores[:, j, :].rearrange("p (h c) -> p h c", c=KEYS),
                                          mx[:, 8 * j:8 * j + 8].unsqueeze(2).to_broadcast([128, 8, KEYS]), ALU.subtract).then_inc(s["shifted"], 1)
                if runs(t, 4):
                    dve.wait_ge(s["proj_done"], b + 1)
                    need(dve, s["h2_out"], 32 * b)
                    dve.scalar_tensor_tensor(out=h2[:].rearrange("p n c -> p (n c)"), in0=far[0:ROWS, 0:2 * D], scalar=1.0 / WS,
                                             in1=h1[k][:].rearrange("p n c -> p (n c)"), op0=ALU.mult, op1=ALU.add).then_inc(s["h2_set"], 1)
                    dve.wait_ge(s["h2_set"], b + 1)
                    need(dve, s["rstd2"], b)
                    statistics(h2, st2, mv2, s["stats2"], s["aggr2"], b + 1)
                if runs(t, 1):
                    dve.wait_ge(s["qk_hi_set"], g + 1)
                    need(dve, s["k_diag_set"], 16 * HPG * g)
                    dve.scalar_tensor_tensor(out=k_st[:], in0=qk_hi[:, :, 1, REACH:REACH + SPAN], scalar=low[:, 0:1],
                                             in1=wide[:, :, SPAN:2 * SPAN], op0=ALU.mult, op1=ALU.add).then_inc(s["k_st_set"], 1)
                    dve.tensor_tensor(q_lo[:, :, REACH:REACH + SPAN], wide[:, :, 0:SPAN], qk_hi[:, :, 0, REACH:REACH + SPAN],
                                      ALU.subtract).then_inc(s["q_lo_set"], 1)
                grp, due = groups(t, k, p, 7)
                if due:
                    route_steps(grp, (k - 7) // 2 % 2, 2)
                if runs(t, 4):
                    dve.wait_ge(s["rstd2"], b + 1)
                    need(dve, s["lo2"], b)
                    normalise(mv2, rs2, xn2, h2).then_inc(s["normed2"], 1)
                grp, due = groups(t, k, p, 7)
                if due:
                    route_steps(grp, (k - 7) // 2 % 2, 3)
                if runs(t, 0):
                    dve.wait_ge(s["embedded"], f + 1)
                    dve.tensor_tensor(h1[k][:], near[0:ROWS, 0:2 * D].rearrange("p (n c) -> p n c", n=2), tab[:],
                                      ALU.add).then_inc(s["h1_set"], 1)
                    dve.wait_ge(s["h1_set"], f + 1)
                    need(dve, s["rstd1"], f)
                    statistics(h1[k], st1, mv1, s["stats1"], s["aggr1"], f + 1)
                grp, due = groups(t, k, p, 6)
                if due:
                    route_steps(grp, (k - 6) // 2 % 2, 0)
                if runs(t, 1):
                    dve.wait_ge(s["v_hi_set"], g + 1)
                    for half in range(2):
                        high, src = value_halves(v_hi[(k - 1) % 4], half)
                        ins = dve.tensor_tensor(value_halves(v_lo[(k - 1) % 4], half)[0], src, high, ALU.subtract)
                    ins.then_inc(s["v_lo_set"], 1)
                if runs(t, 0):
                    dve.wait_ge(s["rstd1"], f + 1)
                    need(dve, s["lo1"], f)
                    normalise(mv1, rs1, xn1, h1[k]).then_inc(s["normed1"], 1)
                if isinstance(t, int) and t == 0:
                    for n, name in enumerate(weights32):
                        dve.wait_ge(s["weights"], n + 1)
                        hi, lo = weights16[name]
                        dve.scalar_tensor_tensor(out=lo[:], in0=weights32[name][:, 0:2, :], scalar=WS, in1=hi[:, 0:2, :],
                                                 op0=ALU.mult, op1=ALU.subtract)
                    dve.wait_ge(s["weights"], 6)
                    dve.scalar_tensor_tensor(out=bp[32:33, :], in0=bp32[32:33, :], scalar=WS, in1=bp[32:33, :],
                                             op0=ALU.mult, op1=ALU.subtract).then_inc(s["setup2"], 1)
                if runs(t, 3):
                    dve.wait_ge(s["pv_done"], c + 1)
                    o = far[:, 0:2 * HEADS * (DH + 1)].rearrange("p (n h d) -> p n h d", n=2, h=HEADS)
                    dve.reciprocal(rden[:], o[:, :, :, DH]).then_inc(s["den_set"], 1)
                    dve.wait_ge(s["den_set"], c + 1)
                    need(dve, s["o_lo_set"], c)
                    dve.tensor_tensor(on[:].rearrange("p n (h d) -> p n h d", h=HEADS), o[:, :, :, 0:DH],
                                      rden[:].unsqueeze(3).to_broadcast([128, 2, HEADS, DH]), ALU.mult).then_inc(s["norm_done"], 1)
                grp, due = groups(t, k, p, 6)
                if due:
                    route_steps(grp, (k - 6) // 2 % 2, 1)
                e = expert_loaded(t)
                if e is not None:
                    dve.wait_ge(s["split_hi"], e + 1)
                    dve.scalar_tensor_tensor(out=w1s[1][:, e], in0=stage1[:, 0:2, :], scalar=WS, in1=w1s[0][:, e, 0:2, :],
                                             op0=ALU.mult, op1=ALU.subtract)
                    dve.scalar_tensor_tensor(out=w2s[1][:, e], in0=stage2[:], scalar=WS, in1=w2s[0][:, e],
                                             op0=ALU.mult, op1=ALU.subtract).then_inc(s["split_lo"], 1)

            pipeline(dve, body)
            last_end = region_end[IMGS // CHOSEN % 2]
            dve.wait_ge(s["later_in"], 64)
            dve.tensor_copy(end_i, last_end[0:1, :]).then_inc(s["end_set"], 1)
            steps = [0]

            def then(ins):
                steps[0] += 1
                ins.then_inc(s["table_step"], 1)
                dve.wait_ge(s["table_step"], steps[0])

            then(dve.tensor_tensor(count, last_end[0:1, :], base, ALU.subtract))
            then(dve.tensor_scalar(count_i, count, float(BATCH - 1), None, ALU.add))
            then(dve.tensor_scalar(count_i, count_i, BATCH.bit_length() - 1, None, ALU.logical_shift_right))
            then(dve.tensor_copy(count, count_i))
            then(dve.memset(ends[:, 0:1], 0.0))
            for e in range(EXPERTS):
                then(dve.tensor_tensor(ends[:, e + 1:e + 2], ends[:, e:e + 1], count[:, e:e + 1], ALU.add))
            then(dve.scalar_tensor_tensor(out=first, in0=ends[:, 0:EXPERTS], scalar=-float(BATCH), in1=base, op0=ALU.mult, op1=ALU.add))
            then(dve.tensor_scalar(first, first, -float(SPARE), None, ALU.add))
            each = number.unsqueeze(2).to_broadcast(MAP)
            then(dve.tensor_tensor(begun, each, ends[:, 0:EXPERTS].unsqueeze(1).to_broadcast(MAP), ALU.is_ge))
            then(dve.tensor_tensor(passed, each, ends[:, 1:EXPERTS + 1].unsqueeze(1).to_broadcast(MAP), ALU.is_ge))
            then(dve.tensor_reduce(sums[0], passed, AX.X, ALU.add))
            then(dve.tensor_scalar(batch_expert[:], sums[0], float(EXPERTS - 1), None, ALU.min))
            then(dve.tensor_tensor(begun, begun, passed, ALU.subtract))
            then(dve.tensor_reduce(sums[1], begun, AX.X, ALU.add))
            then(dve.tensor_tensor(begun, begun, first.unsqueeze(1).to_broadcast(MAP), ALU.mult))
            then(dve.tensor_reduce(sums[2], begun, AX.X, ALU.add))
            then(dve.tensor_tensor(sums[1], sums[1], number, ALU.mult))
            then(dve.scalar_tensor_tensor(out=sums[2], in0=sums[1], scalar=float(BATCH), in1=sums[2], op0=ALU.mult, op1=ALU.add))
            then(dve.tensor_scalar(batch_row[:], sums[2], float(SPARE), None, ALU.add))

        @block.tensor
        def _(pe):
            def turn(src, dst):
                rows, pitch = src.shape[0], max(src.shape[0], PITCH)
                for n in range(2):
                    for c in range(3):
                        at = (3 * n + c) * pitch
                        ins = pe.transpose(dst[:, at:at + rows], src[:, n, 128 * c:128 * c + 128], ident16[0:rows, 0:rows])
                return ins

            def body(t, k, p):
                f, g, a, c, b, r = (t - n for n in range(6))
                if isinstance(t, int) and t == 1:
                    pe.wait_ge(s["zero_mem"], 3)
                    pe.wait_ge(s["setup2"], 2)
                if isinstance(t, int) and t == 0:
                    pe.wait_ge(s["first_in"], 48)
                if runs(t, 3):
                    pe.wait_ge(s["exp_set"], c + 1)
                    pe.wait_ge(s["q_lo_set"], images(g))
                    for m in range(HEADS):
                        ins = pe.transpose(wide[:, m // 4, m % 4 * 128:m % 4 * 128 + 128],
                                           prob[:, 2 * m:2 * m + 2, :].rearrange("p h c -> p (h c)"), identf[:])
                        if m % 4 == 3:
                            ins.then_inc(s["prob_turned"], 1)
                if runs(t, 2):
                    pe.wait_ge(s["k_diag_set"], 16 * HPG * (a + 1))
                    pe.wait_ge(s["q_lo_set"], a + 1)
                    pe.wait_ge(s["v_lo_set"], a + 1)
                    before, counted = groups(t, k, p, 8)
                    if counted:
                        pe.wait_ge(s["step"], STEPS * before + COUNTS_READ)
                    for j in range(GROUPS):
                        for pair in range(2):
                            cols = slice(pair * HPG * KEYS, (pair + 1) * HPG * KEYS)
                            pe.matmul(scores[:, j, cols], identb[:], bandb[:, pair, :].unsqueeze(1).to_broadcast([128, HPG, KEYS]),
                                      start=True, stop=False)
                            for half in range(2):
                                at = QUERIES * (2 * pair + half)
                                dst = scores[64 * half:64 * half + 64, j, cols]
                                keys = k_diag[:, j, :, at:at + KEYS]
                                pe.matmul(dst, qk_hi[:, j, 0, at + REACH:at + REACH + 64], keys, start=False, stop=False)
                                ins = pe.matmul(dst, q_lo[:, j, at + REACH:at + REACH + 64], keys, start=False, stop=True)
                        ins.then_inc(s["scored"], 1)
                if runs(t, 1):
                    pe.wait_ge(s["lo1"], g + 1)
                    need(pe, s["xT2_set"], b)
                    turn(xs1, near[:].bitcast(F16)).then_inc(s["turned1"], 1)
                if runs(t, 5):
                    pe.wait_ge(s["xT2_set"], r + 1)
                    pe.wait_ge(s["norm_done"], images(c))
                    for n in range(2):
                        for j, (x, w, half) in enumerate(PRODUCTS):
                            ins = pe.matmul(far[0:ROWS, n * EXPERTS:(n + 1) * EXPERTS], xT2[:, n, x, :], wr[half][:, w, :],
                                            start=(j == 0), stop=(j == len(PRODUCTS) - 1))
                    ins.then_inc(s["routed"], 1)
                if runs(t, 4):
                    pe.wait_ge(s["o_lo_set"], b + 1)
                    if runs(t, 5):
                        pe.wait_ge(s["logit_set"], r + 1)
                    turn(os_, far[:].bitcast(F16)).then_inc(s["o_turned"], 1)
                if runs(t, 1):
                    pe.wait_ge(s["xT_set"], g + 1)
                    need(pe, s["p_lo_set"], GROUPS * (c + 1))
                    for j in range(GROUPS):
                        for which in range(2):
                            for i, (x, w, half) in enumerate(PRODUCTS):
                                col = (which * GROUPS + j) * 128
                                ins = pe.matmul(wide[:, j, which * SPAN:(which + 1) * SPAN], wqk[half][:, w, col:col + 128],
                                                xT1[:, x, REACH:REACH + SPAN], start=(i == 0), stop=(i == len(PRODUCTS) - 1))
                    ins.then_inc(s["qk_done"], 1)
                if runs(t, 4):
                    pe.wait_ge(s["oT_set"], b + 1)
                    for n in range(2):
                        dst = far[0:ROWS, n * D:n * D + D]
                        pe.matmul(dst, ones16[:, 0:ROWS], bp[:], start=True, stop=False)
                        for j, (x, w, half) in enumerate(PRODUCTS):
                            ins = pe.matmul(dst, oT[:, n, x, :], wp[half][:, w, :], start=False, stop=(j == len(PRODUCTS) - 1))
                    ins.then_inc(s["proj_done"], 1)
                grp, counts = groups(t, k, p, 7)
                if counts:
                    pe.wait_ge(s["marks_set"], grp + 1)
                    pe.wait_ge(s["shifted"], GROUPS * images(a + 1))
                    for n in range(5):
                        dst = scores[0:ROWS, 2, n * EXPERTS:(n + 1) * EXPERTS]
                        for i in range(min(n + 1, 4)):
                            rows = TILE_ROWS[i % 2]
                            ins = pe.matmul(dst, (above16 if i == n else ones16)[0:rows, 0:ROWS], marks[0:rows, i, :],
                                            start=(i == 0), stop=(i == min(n, 3)))
                    ins.then_inc(s["counted"], 1)
                if runs(t, 0):
                    pe.wait_ge(s_patch[k % 2], 16 + 8 * (f - k % 2))
                    for n in range(2):
                        for x in range(KIN):
                            ins = pe.matmul(near[0:ROWS, n * D:n * D + D], patches[k % 2][:, x, n * ROWS:n * ROWS + ROWS],
                                            we[:, x, :], start=(x == 0), stop=(x == KIN - 1))
                    ins.then_inc(s["embedded"], 1)
                if runs(t, 1):
                    pe.wait_ge(s["xV_set"], g + 1)
                    need(pe, s["shifted"], GROUPS * images(a + 1))
                    for i in range(WINDOWS):
                        dst = scores[:, i // 2, i % 2 * D:i % 2 * D + D]
                        for j, (x, w, half) in enumerate(PRODUCTS):
                            ins = pe.matmul(dst, xV[:, x, i, :, :].rearrange("p h c -> p (h c)"), wv[half][:, w, :], start=(j == 0), stop=(j == len(PRODUCTS) - 1))
                    ins.then_inc(s["v_done"], 1)
                if runs(t, 3):
                    pe.wait_ge(s["p_lo_set"], GROUPS * (c + 1))
                    if runs(t, 4):
                        pe.wait_ge(s["h2_set"], b + 1)
                    high, low_v = v_hi[(k - 3) % 4], v_lo[(k - 3) % 4]
                    for pair in range(2):
                        for half in range(2):
                            i, q = 2 * pair + half, slice(64 * half, 64 * half + 64)
                            for h in range(HEADS // 2):
                                m = h // 2 * 4 + pair * 2 + h % 2
                                at = (pair * HEADS // 2 + h) * 2 * (DH + 1)
                                dst = far[q, at:at + 2 * (DH + 1)]
                                pe.matmul(dst, pT_hi[:, m, q], high[:, i, h, :], start=True, stop=False)
                                pe.matmul(dst, pT_hi[:, m, q], low_v[:, i, h, :], start=False, stop=False)
                                ins = pe.matmul(dst, pT_lo[:, m, q], high[:, i, h, :], start=False, stop=True)
                    ins.then_inc(s["pv_done"], 1)
                if runs(t, 4):
                    pe.wait_ge(s["lo2"], b + 1)
                    if runs(t, 0):
                        pe.wait_ge(s["h1_set"], f + 1)
                    turn(payload[:, 2 * k:2 * k + 2, :].bitcast(F16), near[:].bitcast(F16)).then_inc(s["turned2"], 1)

            pipeline(pe, body)


def batch_pipeline(eng, body):
    for u in range(4):
        body(u, u, 0)
    with eng.Fori(1, BATCHES // 4) as p:
        for k in range(4):
            body(4 * p + k, k, p)
    for u in range(BATCHES - 2, BATCHES):
        body(u, u % 4, u // 4)


def experts_part(nc, sorted_dram, batch_row, batch_expert, ident16, w1s, w2s, b1s, b2, out):
    with ExitStack() as ctx:
        def sb(name, shape, dt):
            return ctx.enter_context(nc.sbuf_tensor(name, shape, dt))

        def pb(name, shape, dt):
            return ctx.enter_context(nc.psum_tensor(name, shape, dt))

        def sem(name):
            return ctx.enter_context(nc.semaphore(name))

        rows = [sb(f"rows{k}", [128, PARTS, PAYLOAD], U16) for k in range(4)]
        token = [sb(f"token{k}", [128, PARTS], U32) for k in range(4)]
        weight = [sb(f"weight{k}", [128, PARTS], F32) for k in range(4)]
        b2s = sb("b2s", [128, EXPERTS, D], F32)
        bias2 = [sb(f"bias2_{k}", [128, D], F32) for k in range(4)]
        bias = [sb(f"bias{k}", [128, MF], F32) for k in range(2)]
        xT = [sb(f"e_xT{k}", [128, PARTS, 3, 128], F16) for k in range(2)]
        act_out = sb("act_out", [128, MF, BATCH], F32)
        g_hi = [sb(f"g_hi{k}", [128, MF, BATCH], F16) for k in range(2)]
        g_lo = [sb(f"g_lo{k}", [128, MF, BATCH], F16) for k in range(2)]
        y = [sb(f"y{k}", [128, PARTS, D], F32) for k in range(2)]
        carrier = sb("e_carrier", [32, 2], F32)
        up = [pb(f"up{k}", [128, BATCH], F32) for k in range(3)]
        down = pb("down", [128, 2, 512], F32)
        turned = pb("turned", [128, 2, 512], F32)
        s = {n: sem("e_" + n) for n in "turned xT_set up_done gelu_done hi_done lo_done down_done y_set biased meta_set memory carried b2_in".split()}
        s_rows = [sem(f"e_rows{k}") for k in range(4)]
        s_sent = [sem(f"e_sent{k}") for k in range(2)]
        SENT = 16 * PARTS
        block = ctx.enter_context(nc.Block())

        def last(u, back=0):
            return isinstance(u, int) and u >= BATCHES - 1 - back

        def expert_of(eng, u):
            at = batch_expert[0:1, u:u + 1] if isinstance(u, int) else batch_expert[0:1, bass.ds(u, 1)]
            return eng.value_load(at, min_val=0, max_val=EXPERTS - 1)

        @block.sync
        def _(sp):
            def load(u, k):
                at = batch_row[0:1, u:u + 1] if isinstance(u, int) else batch_row[0:1, bass.ds(u, 1)]
                row = sp.value_load(at, min_val=0, max_val=SPARE)
                sp.dma_start(rows[k][:], sorted_dram[bass.ds(row, BATCH), :].rearrange("(p r) c -> p r c", r=PARTS))\
                  .then_inc(s_rows[k], 16)

            load(0, 0)
            load(1, 1)
            sp.dma_start(b2s[:], b2.to_broadcast([128, EXPERTS, D])).then_inc(s["b2_in"], 16)

            def body(u, k, p):
                if not last(u, 1):
                    need(sp, s["turned"], u - 1)
                    need(sp, s["meta_set"], u - 1)
                    load(u + 2, (k + 2) % 4)

            batch_pipeline(sp, body)

        @block.gpsimd
        def _(pool):
            pool.memset(carrier[:], 0.0).then_inc(s["memory"], 1)
            pool.wait_ge(s["memory"], 1)

            def body(u, k, p):
                pool.wait_ge(s["y_set"], u + 1)
                need(pool, s_sent[1 - k % 2], SENT * (2 * p + (k + 1) // 2))
                need(pool, s["carried"], u)
                pool.tensor_tensor(carrier[:, 1:2], carrier[:, 0:1], carrier[:, 0:1], ALU.mult).then_inc(s["carried"], 1)
                for n in range(PARTS):
                    pool.indirect_dma_start(out=out, out_offset=bass.IndirectOffsetOnAxis(ap=token[k][:, n:n + 1], axis=0),
                                            in_=y[k % 2][:, n, :], in_offset=None, compute_op=ALU.add).then_inc(s_sent[k % 2], 16)

            batch_pipeline(pool, body)
            for k in range(2):
                pool.wait_ge(s_sent[k], SENT * BATCHES // 2)

        @block.scalar
        def _(act):
            def take(u, k):
                act.wait_ge(s["turned"], u + 1)
                need(act, s["up_done"], MF * (u - 1))
                act.copy(xT[k % 2][:].rearrange("p (b n) c r -> p b (n c r)", b=2), turned[:].bitcast(F16)[:, :, 0:6 * 128])\
                   .then_inc(s["xT_set"], 1)

            def gelu(u, k):
                act.wait_ge(s["meta_set"], u + 1)
                for m in range(MF):
                    act.wait_ge(s["up_done"], MF * u + m + 1)
                    need(act, s["lo_done"], MF // 2 * (u - 1) + m // 2 + 1)
                    act.activation(act_out[:, m, :], up[m % 3][:], ACT.Gelu, bias=bias[k % 2][:, m:m + 1], scale=1.0 / WS)\
                       .then_inc(s["gelu_done"], 1)

            take(0, 0)
            take(1, 1)
            gelu(0, 0)

            def body(u, k, p):
                if not last(u, 1):
                    take(u + 2, k + 2)
                if not last(u):
                    gelu(u + 1, k + 1)

            batch_pipeline(act, body)

        @block.vector
        def _(dve):
            def meta(u, k):
                e = expert_of(dve, u)
                dve.wait_ge(s_rows[k], 16 * (u // 4 + 1) if isinstance(u, int) else 4 * (u - k) + 16)
                need(dve, s["gelu_done"], MF * (u - 1))
                dve.tensor_scalar(bias[k % 2][:], b1s[:, bass.ds(e, 1), :].rearrange("p a m -> p (a m)"), 0.0, None, ALU.add)
                dve.tensor_scalar(bias2[k][:], b2s[:, bass.ds(e, 1), :].rearrange("p a d -> p (a d)"), WS, None, ALU.mult)
                dve.tensor_scalar(weight[k][:], rows[k][:, :, WEIGHT_AT:PAYLOAD].bitcast(F32)[:, :, bass.ds(e, 1)].rearrange("p n a -> p (n a)"),
                                  0.0, None, ALU.add)
                dve.tensor_copy(token[k][:], rows[k][:, :, NUMBER_AT:WEIGHT_AT].bitcast(U32).rearrange("p n a -> p (n a)"))\
                   .then_inc(s["meta_set"], 1)

            def split(u, k):
                for j in range(MF // 2):
                    m = slice(2 * j, 2 * j + 2)
                    dve.wait_ge(s["gelu_done"], MF * u + 2 * j + 2)
                    need(dve, s["down_done"], u - 1)
                    dve.tensor_copy(g_hi[k % 2][:, m, :], act_out[:, m, :]).then_inc(s["hi_done"], 1)
                    dve.wait_ge(s["hi_done"], MF // 2 * u + j + 1)
                    dve.tensor_tensor(g_lo[k % 2][:, m, :], act_out[:, m, :], g_hi[k % 2][:, m, :], ALU.subtract).then_inc(s["lo_done"], 1)

            dve.wait_ge(s["b2_in"], 16)
            meta(0, 0)
            meta(1, 1)
            split(0, 0)

            def body(u, k, p):
                if not last(u):
                    split(u + 1, k + 1)
                need(dve, s_sent[k % 2], SENT * (2 * p + k // 2))
                if not last(u, 1):
                    meta(u + 2, (k + 2) % 4)
                dve.wait_ge(s["down_done"], u + 1)
                wide = [128, 2, 2, D]
                dst = y[k % 2][:].rearrange("p (b n) c -> p b n c", b=2)
                dve.tensor_tensor(dst, down[:, :, 0:2 * D].rearrange("p b (n c) -> p b n c", n=2),
                                  bias2[k][:].unsqueeze(1).unsqueeze(1).to_broadcast(wide), ALU.add).then_inc(s["biased"], 1)
                dve.wait_ge(s["biased"], u + 1)
                dve.tensor_tensor(dst, dst, weight[k][:].rearrange("p (b n) -> p b n", b=2).unsqueeze(3).to_broadcast(wide),
                                  ALU.mult).then_inc(s["y_set"], 1)

            batch_pipeline(dve, body)

        @block.tensor
        def _(pe):
            def turn(u, k):
                pe.wait_ge(s_rows[k], 16 * (u // 4 + 1) if isinstance(u, int) else 4 * (u - k) + 16)
                need(pe, s["xT_set"], u)
                for n in range(PARTS):
                    for c in range(3):
                        at = (3 * (n % 2) + c) * 128
                        ins = pe.transpose(turned[:, n // 2, :].bitcast(F16)[:, at:at + 128], rows[k][:, n, 128 * c:128 * c + 128].bitcast(F16), ident16[:])
                ins.then_inc(s["turned"], 1)

            def up_product(u, k, e):
                pe.wait_ge(s["xT_set"], u + 1)
                for m in range(MF):
                    need(pe, s["gelu_done"], MF * u + m - 2)
                    for j, (c, w, h) in enumerate(PRODUCTS):
                        ins = pe.matmul(up[m % 3][:], w1s[h][:, bass.ds(e, 1), w, 128 * m:128 * m + 128].rearrange("p a c -> p (a c)"),
                                        xT[k % 2][:, :, c, :], start=(j == 0), stop=(j == len(PRODUCTS) - 1))
                    ins.then_inc(s["up_done"], 1)

            def down_product(u, k, e):
                pe.wait_ge(s["lo_done"], MF // 2 * (u + 1))
                need(pe, s["biased"], u)
                for n in range(PARTS):
                    dst = down[:, n // 2, (n % 2) * D:(n % 2) * D + D]
                    cols = slice(128 * n, 128 * n + 128)
                    for m in range(MF):
                        high, low = (w2s[h][:, bass.ds(e, 1), m, :] for h in range(2))
                        pe.matmul(dst, g_hi[k % 2][:, m, cols], high, start=(m == 0), stop=False)
                        pe.matmul(dst, g_hi[k % 2][:, m, cols], low, start=False, stop=False)
                        ins = pe.matmul(dst, g_lo[k % 2][:, m, cols], high, start=False, stop=(m == MF - 1))
                ins.then_inc(s["down_done"], 1)

            turn(0, 0)
            turn(1, 1)
            up_product(0, 0, expert_of(pe, 0))

            def body(u, k, p):
                if not last(u, 1):
                    turn(u + 2, (k + 2) % 4)
                if not last(u):
                    up_product(u + 1, k + 1, expert_of(pe, u + 1))
                down_product(u, k, expert_of(pe, u))

            batch_pipeline(pe, body)


def lay_out(x, L0_tok_W, L0_tok_b, L0_tok_class_token, L0_tok_pos_embed, L0_attn_w_qkv, L0_attn_w_proj,
            L0_attn_b_proj, L0_ffn_router_w, L0_ffn_w1, L0_ffn_b1, L0_ffn_w2, L0_ffn_b2):
    f = np.float32
    patches = np.asarray(x).reshape(IMGS, CHANS, NPATCH, PATCH, NPATCH, PATCH).transpose(0, 1, 3, 5, 2, 4)
    patches = patches.reshape(IMGS, KIN, 128, SEQ - 1).transpose(0, 2, 1, 3)
    xt = np.zeros((IMGS, 128, KIN, SPAN), f)
    xt[..., 1:SEQ] = patches

    def two_tiles(a):
        a = np.concatenate([a, np.zeros((SPAN - SEQ, D), f)])
        return np.ascontiguousarray(a.reshape(2, ROWS, D).transpose(1, 0, 2))

    def stacked(w):
        return np.ascontiguousarray(np.asarray(w)[np.array(STACK)].transpose(1, 0, 2))

    bias_tab = np.concatenate([np.asarray(L0_tok_class_token), np.repeat(np.asarray(L0_tok_b)[None], SEQ - 1, 0)])
    qkv = np.asarray(L0_attn_w_qkv)
    cols = [which * D + (g * HPG + h) * DH + d for which in range(2) for g in range(GROUPS) for h in range(HPG)
            for _ in range(2) for d in range(DH)]
    r, c = np.arange(128)[:, None], np.arange(KEYS)[None]
    band = []
    for pair in range(2):
        start = QUERIES * (2 * pair + r // 64)
        key, query = start - REACH + c, start + r % 64
        seen = (abs(key - query) <= REACH) & (key >= 0) & (key < SEQ) | (r % 64 >= QUERIES)
        band.append(np.where(seen, 0.0, MASKED))
    band = np.stack(band, 1)
    fill = np.zeros((128, PARTS, PAYLOAD), np.uint16)
    fill[:, :, NUMBER_AT:WEIGHT_AT] = (TOKENS + np.arange(BATCH, dtype=np.uint32)).reshape(128, PARTS, 1).view(np.uint16)
    return {
        "xt": xt,
        "w_embed": np.asarray(L0_tok_W).T.reshape(KIN, 128, D).transpose(1, 0, 2),
        "bias_tab": two_tiles(bias_tab),
        "pos": two_tiles(np.asarray(L0_tok_pos_embed)),
        "w_qk": stacked(qkv[:, cols]),
        "w_v": stacked(qkv[:, 2 * D:]),
        "w_p": stacked(L0_attn_w_proj),
        "b_p": np.asarray(L0_attn_b_proj)[None],
        "router": stacked(np.asarray(L0_ffn_router_w).T),
        "w1": np.stack([stacked(w) for w in np.asarray(L0_ffn_w1)]),
        "b1": np.asarray(L0_ffn_b1).reshape(EXPERTS, MF, 128).transpose(2, 0, 1),
        "w2": np.asarray(L0_ffn_w2).reshape(EXPERTS, MF, 128, D).transpose(0, 2, 1, 3),
        "b2": np.asarray(L0_ffn_b2).reshape(1, EXPERTS, D),
        "ident": np.eye(128, dtype=f),
        "above": np.triu(np.ones((128, 128), f), 1),
        "numbers": np.arange(BATCHES, dtype=f)[None],
        "token_no": (np.arange(ROWS)[:, None, None] + ROWS * np.arange(2)[None, None] + SEQ * np.arange(IMGS)[None, :, None]).astype(np.int16),
        "fill": fill,
        "region_at": np.repeat(REGION * np.arange(EXPERTS, dtype=f)[None], 128, 0),
        "band": band.astype(f),
        "low_rows": -(np.arange(128) % 32 >= DH).astype(f)[:, None],
    }


def kernel(**inputs):
    import concourse.bacc as bacc
    from concourse.bass_utils import run_bass_kernel_spmd

    nc = bacc.Bacc("TRN2", target_bir_lowering=False, num_devices=1)
    arrays, args = {}, {}
    for name, a in lay_out(**inputs).items():
        a = np.ascontiguousarray(a)
        arrays[f"in_{name}"] = a
        args[name] = nc.dram_tensor(f"in_{name}", a.shape, mybir.dt.from_np(a.dtype), kind="ExternalInput").ap()
    args["out"] = nc.dram_tensor("out_0", (TOKENS + BATCH, D), F32, kind="ExternalOutput").ap()
    vit_tower(nc, **args)
    result = run_bass_kernel_spmd(nc, [arrays], core_ids=[0])
    return result.results[0]["out_0"][:TOKENS].reshape(IMGS, SEQ, D)
```
